# Optimizing a Trainium2 kernel written in Bass

```python
import numpy as np
import jax
import jax.numpy as jnp

def _softmax(x, axis=-1):
    return jax.nn.softmax(x, axis=axis)

def _gelu(x):
    return jax.nn.gelu(x, approximate=True)

def _silu(x):
    return jax.nn.silu(x)

def _sigmoid(x):
    return jax.nn.sigmoid(x)

def _layernorm(x, axis=-1, eps=1e-05):
    m = jnp.mean(x, axis=axis, keepdims=True)
    v = jnp.var(x, axis=axis, keepdims=True)
    return (x - m) / jnp.sqrt(v + eps)

def _scatter_add(tgt, idx, src, axis=0):
    return tgt.at[idx].add(src)

def _segment_sum(src, seg, n):
    return jax.ops.segment_sum(src, seg, n)
kernel_name = 'mk_decoder_preln_d1_seqx_r4_42034f'

def setup_inputs(seed: int=0):
    np.random.seed(seed)
    _w = jnp.asarray

    def _rec_inputs():
        import jax
        import jax.numpy as jnp
        _rk = jax.random.key(seed)
        x = 7.22e-05 + 1 * jax.random.normal(jax.random.fold_in(_rk, 1), (16, 512, 256), jnp.float32)
        _lenS = 512 - jax.random.randint(jax.random.fold_in(_rk, 7), (16,), 0, max(1, 512 // 4) + 1, jnp.int32)
        _lenS2 = 64 - jax.random.randint(jax.random.fold_in(_rk, 8), (16,), 0, max(1, 64 // 4) + 1, jnp.int32)
        _ctx_1024P = jax.random.normal(jax.random.fold_in(_rk, 11), (16, 16, 256), jnp.float32)
        _ctx_1024c = jax.random.dirichlet(jax.random.fold_in(_rk, 511), 0.3 * jnp.ones((16,), jnp.float32), (16, 64))
        _ctx_1024t = jnp.einsum('bsk,bkd->bsd', _ctx_1024c, _ctx_1024P)
        _ctx_1024t = _ctx_1024t * jax.lax.rsqrt(jnp.mean(jnp.square(_ctx_1024t)) + 1e-12) * 0.953939
        ctx_1024 = 4.13588e-05 + 0.999923 * (_ctx_1024t + 0.3 * jax.random.normal(jax.random.fold_in(_rk, 611), (16, 64, 256), jnp.float32))
        _validS = jnp.arange(512)[None, :] < _lenS[:, None]
        _validS2 = jnp.arange(64)[None, :] < _lenS2[:, None]
        _causal = jnp.tril(jnp.ones((512, 512), dtype=bool))
        mask_Bx1x1xS2_ik0 = jnp.where(jnp.broadcast_to(_validS2[:, None, None, :], (16, 1, 1, 64)), 0, 1).astype(jnp.int32)
        return (x, ctx_1024, mask_Bx1x1xS2_ik0)
    x, ctx_1024, mask_Bx1x1xS2_ik0 = _rec_inputs()

    def _L0_attn_setup():
        import jax, jax.numpy as jnp
        import numpy as np
        HEADS = 16
        NUM_LANDMARKS = 64
        PINV_ITERS = 6
        D_MODEL = 256

        def _moore_penrose_pinv(x, num_iters):
            m = x.shape[-1]
            I = jnp.eye(m, dtype=x.dtype)
            V = x
            for _ in range(num_iters):
                KV = x @ V
                V = 0.25 * V @ (13.0 * I - KV @ (15.0 * I - KV @ (7.0 * I - KV)))
            return V
        key = jax.random.key(seed)
        k1, k2, k3 = jax.random.split(key, 3)
        b, n, d = (4, 1024, D_MODEL)
        hidden_states = jax.random.normal(k1, (b, n, d), dtype=jnp.float32)
        Wqkv = jax.random.normal(k2, (d, 3 * d), dtype=jnp.float32) * 0.02
        bqkv = jnp.zeros((3 * d,), dtype=jnp.float32)
        Wout = jax.random.normal(k3, (d, d), dtype=jnp.float32) * 0.02
        bout = jnp.zeros((d,), dtype=jnp.float32)
        return {'hidden_states': hidden_states, 'Wqkv': Wqkv, 'bqkv': bqkv, 'Wout': Wout, 'bout': bout}
    _L0_attn_all = _L0_attn_setup()
    _L0_attn_in = {k: v for k, v in _L0_attn_all.items() if k in ('Wqkv', 'bqkv', 'Wout', 'bout')}
    del _L0_attn_all

    def _L0_xattn_setup():
        import jax, jax.numpy as jnp
        import numpy as np
        D_MODEL = 256
        N_HEADS = 16
        HEAD_DIM = D_MODEL // N_HEADS
        B, S = (4, 512)
        NEG = -1000000000.0

        def _split_heads(x):
            b, s, _ = x.shape
            return x.reshape(b, s, N_HEADS, HEAD_DIM).transpose(0, 2, 1, 3)
        key = jax.random.key(seed)
        ks = jax.random.split(key, 13)
        sc = 1.0 / np.sqrt(D_MODEL)
        return {'query': jax.random.normal(ks[0], (B, S, D_MODEL), jnp.float32), 'key': jax.random.normal(ks[1], (B, S, D_MODEL), jnp.float32), 'value': jax.random.normal(ks[2], (B, S, D_MODEL), jnp.float32), 'mask': jax.random.randint(ks[3], (B, 1, 1, S), 0, 2, jnp.int32), 'Wq': jax.random.normal(ks[4], (D_MODEL, D_MODEL), jnp.float32) * sc, 'bq': jax.random.normal(ks[5], (D_MODEL,), jnp.float32) * sc, 'Wk': jax.random.normal(ks[6], (D_MODEL, D_MODEL), jnp.float32) * sc, 'bk': jax.random.normal(ks[7], (D_MODEL,), jnp.float32) * sc, 'Wv': jax.random.normal(ks[8], (D_MODEL, D_MODEL), jnp.float32) * sc, 'bv': jax.random.normal(ks[9], (D_MODEL,), jnp.float32) * sc, 'Wo': jax.random.normal(ks[10], (D_MODEL, D_MODEL), jnp.float32) * sc, 'bo': jax.random.normal(ks[11], (D_MODEL,), jnp.float32) * sc}
    _L0_xattn_all = _L0_xattn_setup()
    _L0_xattn_in = {k: v for k, v in _L0_xattn_all.items() if k in ('Wq', 'bq', 'Wk', 'bk', 'Wv', 'bv', 'Wo', 'bo')}
    del _L0_xattn_all

    def _L0_ffn_setup():
        import jax, jax.numpy as jnp
        import numpy as np
        B, S, H = (8, 1024, 256)
        NAV = 128
        E = 8
        F = 2 * H
        key = jax.random.key(seed)
        ks = jax.random.split(key, 12)

        def w(k, shape, fan_in):
            return jax.random.normal(k, shape, dtype=jnp.float32) / np.sqrt(fan_in)
        return {'hidden_states': jax.random.normal(ks[0], (B, S, H), dtype=jnp.float32), 'Wp1': w(ks[1], (H, NAV), H), 'bp1': jnp.zeros((NAV,), jnp.float32), 'Wp2': w(ks[2], (NAV, E), NAV), 'bp2': jnp.zeros((E,), jnp.float32), 'W1': w(ks[3], (E, H, F), H), 'b1': jnp.zeros((E, F), jnp.float32), 'W2': w(ks[4], (E, F, H), F), 'b2': jnp.zeros((E, H), jnp.float32), 'Wo': w(ks[5], (H, H), H), 'bo': jnp.zeros((H,), jnp.float32)}
    _L0_ffn_all = _L0_ffn_setup()
    _L0_ffn_in = {k: v for k, v in _L0_ffn_all.items() if k in ('Wp1', 'bp1', 'Wp2', 'bp2', 'W1', 'b1', 'W2', 'b2', 'Wo', 'bo')}
    del _L0_ffn_all
    return {'x': x, 'ctx_1024': ctx_1024, 'mask_Bx1x1xS2_ik0': mask_Bx1x1xS2_ik0, 'L0_attn_Wqkv': _L0_attn_in['Wqkv'], 'L0_attn_bqkv': _L0_attn_in['bqkv'], 'L0_attn_Wout': _L0_attn_in['Wout'], 'L0_attn_bout': _L0_attn_in['bout'], 'L0_xattn_Wq': _L0_xattn_in['Wq'], 'L0_xattn_bq': _L0_xattn_in['bq'], 'L0_xattn_Wk': _L0_xattn_in['Wk'], 'L0_xattn_bk': _L0_xattn_in['bk'], 'L0_xattn_Wv': _L0_xattn_in['Wv'], 'L0_xattn_bv': _L0_xattn_in['bv'], 'L0_xattn_Wo': _L0_xattn_in['Wo'], 'L0_xattn_bo': _L0_xattn_in['bo'], 'L0_ffn_Wp1': _L0_ffn_in['Wp1'], 'L0_ffn_bp1': _L0_ffn_in['bp1'], 'L0_ffn_Wp2': _L0_ffn_in['Wp2'], 'L0_ffn_bp2': _L0_ffn_in['bp2'], 'L0_ffn_W1': _L0_ffn_in['W1'], 'L0_ffn_b1': _L0_ffn_in['b1'], 'L0_ffn_W2': _L0_ffn_in['W2'], 'L0_ffn_b2': _L0_ffn_in['b2'], 'L0_ffn_Wo': _L0_ffn_in['Wo'], 'L0_ffn_bo': _L0_ffn_in['bo']}

def reference(x, ctx_1024, mask_Bx1x1xS2_ik0, L0_attn_Wqkv, L0_attn_bqkv, L0_attn_Wout, L0_attn_bout, L0_xattn_Wq, L0_xattn_bq, L0_xattn_Wk, L0_xattn_bk, L0_xattn_Wv, L0_xattn_bv, L0_xattn_Wo, L0_xattn_bo, L0_ffn_Wp1, L0_ffn_bp1, L0_ffn_Wp2, L0_ffn_bp2, L0_ffn_W1, L0_ffn_b1, L0_ffn_W2, L0_ffn_b2, L0_ffn_Wo, L0_ffn_bo):
    import jax
    import jax.numpy as jnp

    def _L0_attn_ref(hidden_states, Wqkv, bqkv, Wout, bout):
        import jax, jax.numpy as jnp
        import numpy as np
        HEADS = 16
        NUM_LANDMARKS = 64
        PINV_ITERS = 6
        D_MODEL = 256

        def _moore_penrose_pinv(x, num_iters):
            m = x.shape[-1]
            I = jnp.eye(m, dtype=x.dtype)
            V = x
            for _ in range(num_iters):
                KV = x @ V
                V = 0.25 * V @ (13.0 * I - KV @ (15.0 * I - KV @ (7.0 * I - KV)))
            return V
        b, n, d = hidden_states.shape
        h, m = (HEADS, NUM_LANDMARKS)
        dh = d // h
        scale = 1.0 / np.sqrt(dh).astype(np.float32)
        l = n // m
        qkv = hidden_states @ Wqkv + bqkv
        q, k, v = jnp.split(qkv, 3, axis=-1)

        def to_heads(t):
            return t.reshape(b, n, h, dh).transpose(0, 2, 1, 3)
        q, k, v = (to_heads(q), to_heads(k), to_heads(v))
        q = q * scale
        q_l = q.reshape(b, h, m, l, dh).mean(axis=3)
        k_l = k.reshape(b, h, m, l, dh).mean(axis=3)
        sim1 = jnp.einsum('bhid,bhjd->bhij', q, k_l)
        sim2 = jnp.einsum('bhid,bhjd->bhij', q_l, k_l)
        sim3 = jnp.einsum('bhid,bhjd->bhij', q_l, k)
        attn1 = jax.nn.softmax(sim1, axis=-1)
        attn2 = jax.nn.softmax(sim2, axis=-1)
        attn3 = jax.nn.softmax(sim3, axis=-1)
        attn2_inv = _moore_penrose_pinv(attn2, PINV_ITERS)
        out = attn1 @ (attn2_inv @ (attn3 @ v))
        out = out.transpose(0, 2, 1, 3).reshape(b, n, d)
        out = out @ Wout + bout
        return out

    def _L0_xattn_ref(query, key, value, mask, Wq, bq, Wk, bk, Wv, bv, Wo, bo):
        import jax, jax.numpy as jnp
        import numpy as np
        D_MODEL = 256
        N_HEADS = 16
        HEAD_DIM = D_MODEL // N_HEADS
        B, S = (4, 512)
        NEG = -1000000000.0

        def _split_heads(x):
            b, s, _ = x.shape
            return x.reshape(b, s, N_HEADS, HEAD_DIM).transpose(0, 2, 1, 3)
        Q = _split_heads(query @ Wq.T + bq)
        K = _split_heads(key @ Wk.T + bk)
        V = _split_heads(value @ Wv.T + bv)
        scores = jnp.einsum('bhqd,bhkd->bhqk', Q, K) / np.sqrt(HEAD_DIM)
        scores = jnp.where(mask == 0, NEG, scores)
        probs = jax.nn.softmax(scores, axis=-1)
        ctx = jnp.einsum('bhqk,bhkd->bhqd', probs, V)
        ctx = ctx.transpose(0, 2, 1, 3).reshape(query.shape[0], query.shape[1], D_MODEL)
        return ctx @ Wo.T + bo

    def _L0_ffn_ref(hidden_states, Wp1, bp1, Wp2, bp2, W1, b1, W2, b2, Wo, bo):
        import jax, jax.numpy as jnp
        import numpy as np
        B, S, H = (8, 1024, 256)
        NAV = 128
        E = 8
        F = 2 * H
        last = hidden_states[:, -1, :]
        logits = jax.nn.gelu(last @ Wp1 + bp1, approximate=False) @ Wp2 + bp2
        action_probs = jax.nn.softmax(logits, axis=-1)
        sel = jnp.argmax(action_probs, axis=-1)
        w1 = W1[sel]
        w2 = W2[sel]
        h = jax.nn.gelu(jnp.einsum('bsh,bhf->bsf', hidden_states, w1) + b1[sel][:, None, :], approximate=False)
        reasoned = jnp.einsum('bsf,bfh->bsh', h, w2) + b2[sel][:, None, :]
        out = reasoned @ Wo + bo
        return hidden_states + 0.3 * out
    x = x + _L0_attn_ref(_layernorm(x, axis=-1), L0_attn_Wqkv, L0_attn_bqkv, L0_attn_Wout, L0_attn_bout)
    x = x + _L0_xattn_ref(_layernorm(x, axis=-1), ctx_1024, ctx_1024, mask_Bx1x1xS2_ik0, L0_xattn_Wq, L0_xattn_bq, L0_xattn_Wk, L0_xattn_bk, L0_xattn_Wv, L0_xattn_bv, L0_xattn_Wo, L0_xattn_bo)
    x = x + _L0_ffn_ref(_layernorm(x, axis=-1), L0_ffn_Wp1, L0_ffn_bp1, L0_ffn_Wp2, L0_ffn_bp2, L0_ffn_W1, L0_ffn_b1, L0_ffn_W2, L0_ffn_b2, L0_ffn_Wo, L0_ffn_bo)
    return x

_drawn_inputs = setup_inputs


def setup_inputs(seed=0):
    import zlib

    import numpy as np

    out = dict(_drawn_inputs(seed))
    spreads = {'L0_attn_bqkv': (0.0, 0.1),
     'L0_attn_bout': (0.0, 0.1),
     'L0_ffn_bp1': (0.0, 0.1),
     'L0_ffn_bp2': (0.0, 0.1),
     'L0_ffn_b1': (0.0, 0.1),
     'L0_ffn_b2': (0.0, 0.1),
     'L0_ffn_bo': (0.0, 0.1)}
    factors = {}
    for name, (base, spread) in spreads.items():
        noise = np.random.default_rng([zlib.crc32(name.encode()), seed]).standard_normal(out[name].shape)
        drawn = base * np.exp(spread * noise) if base else spread * noise
        out[name] = jnp.asarray(drawn.astype(out[name].dtype))
    for name, factor in factors.items():
        out[name] = (out[name] * factor).astype(out[name].dtype)
    return out
```

```python
from contextlib import ExitStack

import concourse.bass as bass
from concourse import mybir

ALU = mybir.AluOpType
ACT = mybir.ActivationFunctionType
AX = mybir.AxisListType
F32 = mybir.dt.float32
BF16 = mybir.dt.bfloat16
I32 = mybir.dt.int32
U32 = mybir.dt.uint32

P = 128
HEADS = 16
DH = 16
LM = 64
PAIRS = HEADS // 2
ITERS = 6
BANKS = 8
EPS = 1e-5
NEG_PARTS = (-998244352.0, -1753088.0, -2560.0)
assert sum(NEG_PARTS) == -1e9


def step_order():
    s = [("kx", 0), ("vx", 0), ("xnT", 0), ("xnT", 1)]
    s += [("q", 0), ("q", 1), ("k", 0), ("k", 1), ("v", 0), ("v", 1)]
    s += [("s2", 0), ("s3", 0), ("s3", 1), ("s3", 2), ("x2T", 0)]
    s += [("s3", 3), ("p3T", 0), ("s3", 4), ("p3T", 1), ("a", 0), ("a", 1)]
    s += [("s3", 5), ("p3T", 2), ("s3", 6), ("p3T", 3), ("s3", 7)]
    s += [("p3T", p) for p in range(4, 8)] + [("z", 0)]
    fillers = []
    for n in range(8):
        fillers.append(("s1", n))
        if n >= 1:
            fillers.append(("p1T", n - 1))
    fillers.append(("p1T", 7))
    for it in range(ITERS):
        for part in ("ps", "pe"):
            s += [(part, it, 0), (part, it, 1)]
            if fillers:
                s.append(fillers.pop(0))
        for h in range(2):
            if it < ITERS - 1:
                s.append(("put", it, h))
            s.append(("puz", it, h))
            if h and fillers:
                s.append(fillers.pop(0))
    s += [("y", 0)]
    s += fillers
    s += [("den1", 0), ("o1", 0), ("den1", 1), ("o1", 1), ("w1", 0), ("w1", 1)]
    s += [("xnT", 2), ("xnT", 3), ("qx", 0), ("qx", 1)]
    for n in range(8):
        s.append(("sx", n))
        if n >= 2:
            s.append(("pxT", n - 2))
    s += [("pxT", 6), ("pxT", 7)]
    s += [("denx", 0), ("ox", 0), ("denx", 1), ("ox", 1), ("wx", 0), ("wx", 1)]
    s += [("xnT", 4), ("xnT", 5), ("gate", 0), ("logit", 0)]
    s += [("h", m) for m in range(4)] + [("r", 0), ("r", 1), ("y3", 0), ("y3", 1)]
    return s


STEPS = step_order()
FILL = {name: n for n, name in enumerate(STEPS)}
assert len(FILL) == len(STEPS)
NF = len(STEPS)
USES = [len(range(b, NF, BANKS)) for b in range(BANKS)]


class Signal:

    def __init__(self, sem, per):
        self.sem, self.per = sem, per

    def at(self, i, k):
        return (i + 1) * self.per + k

    def before(self, i, k):
        return i * self.per + k


def decoder_kernel(nc, a, out):
    B, S, D = a["x"].shape
    T = S // P
    KD = D // P
    FF = 512
    FM = FF // P
    LSEG = S // LM
    QK = 0.25

    with ExitStack() as ctx:
        def sb(name, shape, dt=F32):
            return ctx.enter_context(nc.sbuf_tensor(name, shape, dt))

        def sem(name):
            return ctx.enter_context(nc.semaphore(name))

        bank = [ctx.enter_context(nc.psum_tensor(f"bank{b}", [P, 512], F32)) for b in range(BANKS)]

        wqkv = sb("wqkv", [P, KD, 3 * D])
        wout = sb("wout", [P, KD, D])
        wq = sb("wq", [P, KD, D])
        wk = sb("wk", [P, KD, D])
        wv = sb("wv", [P, KD, D])
        wo = sb("wo", [P, KD, D])
        wp1 = sb("wp1", [P, KD, P])
        wp2 = sb("wp2", [P, 8])
        wfo = sb("wfo", [P, KD, D])
        bqkv_col = sb("bqkv_col", [P, 6])
        bq4_col = sb("bq4_col", [P, 2])
        bqx_col = sb("bqx_col", [P, 2])
        bkx_col = sb("bkx_col", [P, 2])
        bp1_col = sb("bp1_col", [P, 1])
        bp2_row = sb("bp2_row", [1, 8])
        bv_row = sb("bv_row", [P, D])
        bout_row = sb("bout_row", [P, D])
        bvx_row = sb("bvx_row", [P, D])
        box_row = sb("box_row", [P, D])
        bfo_row = sb("bfo_row", [P, D])
        bfo3_row = sb("bfo3_row", [P, D])
        ident = sb("ident", [P, P])
        head_mask = sb("head_mask", [P, 8])
        head_mean = sb("head_mean", [P, 8])
        ones_bd = sb("ones_bd", [P, 32])
        ones3 = sb("ones3", [3, P], BF16)
        neg_col = sb("neg_col", [3, 1])
        x_in = sb("x_in", [P, T, D])
        xr = sb("xr", [P, T, D])
        stats = sb("stats", [P, T, 6])
        mv = sb("mv", [P, T, 2])
        var_eps = sb("var_eps", [P, T])
        minus_half = sb("minus_half", [P, T])
        rstd = sb("rstd", [P, T])
        xn = sb("xn", [P, T, D])
        xnT = sb("xnT", [P, KD, S])
        qT = sb("qT", [P, KD, S])
        kT = sb("kT", [P, KD, S])
        vt = sb("vt", [P, T, D])
        qsum = sb("qsum", [P, KD, LM])
        ksum = sb("ksum", [P, KD, LM])
        qbd = sb("qbd", [P, KD, 8, LM])
        kbd = sb("kbd", [P, KD, 8, LM])
        m2 = sb("m2", [P, PAIRS])
        d2 = sb("d2", [P, PAIRS, LM])
        e2 = sb("e2", [P, PAIRS, LM])
        r2 = sb("r2", [P, PAIRS])
        attn2 = sb("attn2", [P, PAIRS, LM])
        attn2T = sb("attn2T", [P, PAIRS, LM])
        nm3 = sb("nm3", [P, PAIRS])
        sum3 = sb("sum3", [P, PAIRS])
        r3 = sb("r3", [P, PAIRS])
        p3 = sb("p3", [P, 2, S])
        p3T = sb("p3T", [P, PAIRS, T, P])
        uz = sb("uz", [P, PAIRS, LM + DH])
        ut = sb("ut", [P, PAIRS, LM])
        dd = sb("dd", [P, PAIRS, LM])
        gt = sb("gt", [P, PAIRS, LM])
        y_bd = sb("y_bd", [P, PAIRS, 32])
        m1 = sb("m1", [P, 2, 8])
        d1 = sb("d1", [P, 2, 8, LM])
        p1 = sb("p1", [P, 2, 4, P])
        p1T = sb("p1T", [P, PAIRS, S])
        rden = sb("rden", [P, 2, S])
        oT = sb("oT", [P, KD, S])
        x1 = sb("x1", [P, T, D])
        x1b = sb("x1b", [P, T, D])
        ctxT = sb("ctxT", [P, KD, LM])
        mask_in = sb("mask_in", [P, LM], I32)
        key_mask = sb("key_mask", [P, LM])
        neg_row = sb("neg_row", [3, LM], BF16)
        kxT = sb("kxT", [P, KD, LM])
        kx_bd = sb("kx_bd", [P, KD, 8, LM])
        vx_bd = sb("vx_bd", [P, PAIRS, 32])
        qxT = sb("qxT", [P, KD, S])
        x2 = sb("x2", [P, T, D])
        base = sb("base", [P, T, D])
        base2 = sb("base2", [P, T, D])
        gate_h = sb("gate_h", [P, 1])
        logits = sb("logits", [1, 8])
        top8 = sb("top8", [1, 8])
        sel8 = sb("sel8", [1, 8], U32)
        w1e = sb("w1e", [P, KD, FF])
        w2e = sb("w2e", [P, FM, D])
        b1e = sb("b1e", [P, FM])
        b2e = sb("b2e", [P, KD])
        hT = sb("hT", [P, FM, S])
        rT = sb("rT", [P, KD, S])
        yo = sb("yo", [P, T, D])

        filled = Signal(sem("psum_filled"), NF)
        free = [Signal(sem(f"bank{b}_free"), USES[b]) for b in range(BANKS)]
        consts_loaded = sem("consts_loaded")
        x_loaded = Signal(sem("x_loaded"), 16)
        ctx_loaded = Signal(sem("ctx_loaded"), 32)
        expert_loaded = Signal(sem("expert_loaded"), 64)
        stored = Signal(sem("stored"), 16)
        pool_consts = sem("pool_consts")
        dve_consts = sem("dve_consts")
        stats_done = Signal(sem("stats_done"), 3)
        rstd_done = Signal(sem("rstd_done"), 3)
        xn_done = Signal(sem("xn_done"), 3)
        xnT_act = Signal(sem("xnT_act"), 3)
        xnT_dve = Signal(sem("xnT_dve"), 3)
        q_done = Signal(sem("q_done"), 2)
        k_done = Signal(sem("k_done"), 2)
        v_done = Signal(sem("v_done"), 2)
        lm_done = Signal(sem("lm_done"), 2)
        bd_done = Signal(sem("bd_done"), 2)
        d2_done = Signal(sem("d2_done"), 1)
        e2_done = Signal(sem("e2_done"), 1)
        attn2_done = Signal(sem("attn2_done"), 1)
        attn2T_done = Signal(sem("attn2T_done"), 1)
        a_done = Signal(sem("a_done"), 2)
        nm3_done = Signal(sem("nm3_done"), PAIRS)
        p3_done = Signal(sem("p3_done"), PAIRS)
        p3T_done = Signal(sem("p3T_done"), PAIRS)
        z_done = Signal(sem("z_done"), 1)
        dd_done = Signal(sem("dd_done"), 2 * ITERS)
        gt_done = Signal(sem("gt_done"), 2 * ITERS)
        ut_done = Signal(sem("ut_done"), 2 * (ITERS - 1))
        uz_done = Signal(sem("uz_done"), 2 * ITERS)
        y_done = Signal(sem("y_done"), 1)
        d1_done = Signal(sem("d1_done"), 16)
        p1_done = Signal(sem("p1_done"), 16)
        p1T_done = Signal(sem("p1T_done"), 16)
        o_done = Signal(sem("o_done"), 4)
        xres_done = Signal(sem("xres_done"), 3)
        x1_done = Signal(sem("x1_done"), 2)
        x2_done = Signal(sem("x2_done"), 2)
        key_mask_done = Signal(sem("key_mask_done"), 1)
        kx_done = Signal(sem("kx_done"), 1)
        kxbd_done = Signal(sem("kxbd_done"), 1)
        vx_done = Signal(sem("vx_done"), 1)
        qx_done = Signal(sem("qx_done"), 2)
        gate_done = Signal(sem("gate_done"), 1)
        sel_done = Signal(sem("sel_done"), 1)
        h_done = Signal(sem("h_done"), FM)
        r_done = Signal(sem("r_done"), 2)
        yo_done = Signal(sem("yo_done"), 2)
        pe_turn, act_turn = sem("pe_turn"), sem("act_turn")
        pool_turn, sp_turn = sem("pool_turn"), sem("sp_turn")

        dve_makes = [stats_done, xn_done, xnT_dve, k_done, v_done, lm_done, d2_done, attn2_done,
                     nm3_done, z_done, dd_done, gt_done, ut_done, uz_done, y_done, d1_done, o_done,
                     x1_done, x2_done, key_mask_done, kx_done, vx_done, sel_done, r_done, yo_done,
                     attn2T_done, *free]
        act_makes = [xnT_act, q_done, e2_done, a_done, p3_done, p3T_done, p1_done, p1T_done,
                     qx_done, gate_done, h_done]
        pool_makes = [rstd_done, bd_done, xres_done, kxbd_done]

        def tile(step):
            return bank[FILL[step] % BANKS]

        def free_of(step):
            return free[FILL[step] % BANKS].sem

        def full(eng, i, step):
            eng.wait_ge(filled.sem, filled.at(i, FILL[step] + 1))

        def full_before(eng, i, step):
            eng.wait_ge(filled.sem, filled.before(i, FILL[step] + 1))

        block = ctx.enter_context(nc.Block())
        x_dram = a["x"].rearrange("b (t p) d -> p (b t) d", p=P)
        out_dram = out.rearrange("b (t p) d -> p (b t) d", p=P)
        ctx_dram = a["ctxT"].rearrange("b (k p) c -> p (b k) c", p=P)
        mask_dram = a["mask"]
        w1_dram = a["W1"].rearrange("e (k p) f -> p (e k) f", p=P)
        w2_dram = a["W2"].rearrange("e (k p) f -> p (e k) f", p=P)

        def halves(w):
            return w.rearrange("(k p) n -> p k n", p=P)

        CONSTS = [
            (wqkv[:], halves(a["Wqkv"])), (bqkv_col[:], a["bqkv"]), (bv_row[:], a["bv"]),
            (wk[:], halves(a["WkT"])), (wv[:], halves(a["WvT"])), (bkx_col[:], a["bkx"]),
            (bvx_row[:], a["bvx"]), (wout[:], halves(a["Wout"])), (bout_row[:], a["bout"]),
            (wq[:], halves(a["WqT"])), (bqx_col[:], a["bqx"]), (wo[:], halves(a["WoT"])),
            (box_row[:], a["box"]), (wp1[:], halves(a["Wp1"])), (bp1_col[:], a["bp1"]),
            (wp2[:], a["Wp2"]), (bp2_row[:], a["bp2"]), (wfo[:], halves(a["Wfo"])),
            (bfo_row[:], a["bfo"]),
        ]

        @block.sync
        def _(sp):
            def load(i, first=False):
                if not first:
                    sp.wait_ge(xn_done.sem, xn_done.before(i, 1))
                    sp.sem_inc(sp_turn, 1)
                    sp.wait_ge(xres_done.sem, xres_done.before(i, 1))
                    sp.sem_inc(sp_turn, 1)
                sp.dma_start(x_in[:], x_dram[:, bass.ds(i * T, T), :]).then_inc(x_loaded.sem, 16)
                if not first:
                    full_before(sp, i, ("vx", 0))
                    sp.sem_inc(sp_turn, 1)
                    sp.wait_ge(key_mask_done.sem, key_mask_done.before(i, 1))
                    sp.sem_inc(sp_turn, 1)
                sp.dma_start(ctxT[:], ctx_dram[:, bass.ds(i * KD, KD), :]).then_inc(ctx_loaded.sem, 16)
                sp.dma_start(mask_in[:], mask_dram[:, bass.ds(i * LM, LM)]).then_inc(ctx_loaded.sem, 16)

            def store(i):
                sp.wait_ge(yo_done.sem, yo_done.at(i, 2))
                sp.sem_inc(sp_turn, 1)
                sp.dma_start(out_dram[:, bass.ds(i * T, T), :], yo[:]).then_inc(stored.sem, 16)

            sp.sem_inc(x_loaded.sem, 16)
            sp.sem_inc(ctx_loaded.sem, 32)
            sp.sem_inc(stored.sem, 16)
            load(0, first=True)
            for dst, src in CONSTS:
                sp.dma_start(dst, src).then_inc(consts_loaded, 16)
            with sp.Fori(0, B - 1) as i:
                load(i + 1)
                store(i)
            store(B - 1)
            sp.wait_ge(stored.sem, stored.at(B - 1, 16))

        @block.gpsimd
        def _(pool):
            g = nc.gpsimd
            for s in pool_makes:
                pool.sem_inc(s.sem, s.per)
            g.memset(ident[:], 0.0)
            g.memset(head_mask[:], 1.0)
            g.memset(ones_bd[:], 0.0)
            g.memset(neg_col[:], NEG_PARTS[0])
            g.memset(y_bd[:], 0.0)
            g.memset(vx_bd[:], 0.0)
            g.memset(ones3[:], 1.0)
            g.memset(minus_half[:], -0.5)
            g.drain()
            g.affine_select(out=ident[:], in_=ident[:], compare_op=ALU.not_equal, fill=1.0,
                            base=0, pattern=[[-1, P]], channel_multiplier=1)
            g.affine_select(out=head_mask[:], in_=head_mask[:], compare_op=ALU.is_ge, fill=0.0,
                            base=0, pattern=[[-DH, 8]], channel_multiplier=1)
            g.drain()
            g.memset(ones_bd[0:64, 0:16], 1.0)
            g.drain()
            g.memset(ones_bd[64:128, 16:32], 1.0)
            g.drain()
            g.affine_select(out=neg_col[:], in_=neg_col[:], compare_op=ALU.not_equal,
                            fill=NEG_PARTS[1], base=-1, pattern=[[0, 1]], channel_multiplier=1)
            g.drain()
            g.affine_select(out=head_mask[:], in_=head_mask[:], compare_op=ALU.is_ge, fill=0.0,
                            base=DH - 1, pattern=[[DH, 8]], channel_multiplier=-1)
            g.affine_select(out=neg_col[:], in_=neg_col[:], compare_op=ALU.not_equal,
                            fill=NEG_PARTS[2], base=-2, pattern=[[0, 1]], channel_multiplier=1)
            g.drain()
            g.tensor_scalar(head_mean[:], head_mask[:], 1.0 / LSEG, None, ALU.mult)
            g.tensor_scalar(head_mask[:], head_mask[:], QK, None, ALU.mult)
            g.drain().then_inc(pool_consts, 1)
            pool.wait_ge(consts_loaded, 16 * len(CONSTS))
            pool.wait_ge(dve_consts, 1)

            def layer_rstd(i, n):
                pool.wait_ge(stats_done.sem, stats_done.at(i, n + 1))
                pool.sem_inc(pool_turn, 1)
                g.tensor_scalar(var_eps[:], mv[:, :, 1], EPS, None, ALU.add)
                g.drain()
                g.tensor_tensor(rstd[:], var_eps[:], minus_half[:], ALU.pow).then_inc(rstd_done.sem, 1)

            def spread(dst, src, scale):
                return g.tensor_tensor(dst, src.unsqueeze(1).broadcast_to([P, 8, LM]),
                                       scale.unsqueeze(2).broadcast_to([P, 8, LM]), ALU.mult)

            def add_row(dst, src, row):
                return g.tensor_tensor(dst, src, row[:].unsqueeze(1).broadcast_to([P, T, D]), ALU.add)

            with pool.Fori(0, B) as i:
                pool.wait_ge(kx_done.sem, kx_done.at(i, 1))
                full_before(pool, i, ("sx", 7))
                for k in range(KD):
                    last = spread(kx_bd[:, k], kxT[:, k], head_mask[:])
                last.then_inc(kxbd_done.sem, 1)
                layer_rstd(i, 0)
                pool.wait_ge(x_loaded.sem, x_loaded.at(i, 16))
                pool.wait_ge(x1_done.sem, x1_done.before(i, 2))
                add_row(xr[:], x_in[:], bout_row).then_inc(xres_done.sem, 1)
                full_before(pool, i, ("s1", 7))
                pool.wait_ge(lm_done.sem, lm_done.at(i, 1))
                for k in range(KD):
                    last = spread(qbd[:, k], qsum[:, k], head_mean[:])
                last.then_inc(bd_done.sem, 1)
                pool.wait_ge(lm_done.sem, lm_done.at(i, 2))
                for k in range(KD):
                    last = spread(kbd[:, k], ksum[:, k], head_mean[:])
                last.then_inc(bd_done.sem, 1)
                layer_rstd(i, 1)
                pool.wait_ge(x1_done.sem, x1_done.at(i, 2))
                pool.wait_ge(x2_done.sem, x2_done.before(i, 2))
                add_row(x1b[:], x1[:], box_row).then_inc(xres_done.sem, 1)
                layer_rstd(i, 2)
                pool.wait_ge(x2_done.sem, x2_done.at(i, 2))
                pool.wait_ge(yo_done.sem, yo_done.before(i, 2))
                add_row(base[:], x2[:], bfo3_row)
                g.drain()
                pool.wait_ge(xn_done.sem, xn_done.at(i, 3))
                g.tensor_tensor(base2[:], base[:], xn[:], ALU.add).then_inc(xres_done.sem, 1)

        @block.scalar
        def _(act):
            s = nc.scalar
            for sig in act_makes:
                act.sem_inc(sig.sem, sig.per)
            act.sem_inc(expert_loaded.sem, 64)
            act.wait_ge(consts_loaded, 16 * len(CONSTS))
            act.wait_ge(dve_consts, 1)

            def copy(dst, src, sig, step):
                s.activation(dst, src, ACT.Copy).then_inc(free_of(step), 1)
                act.drain().then_inc(sig.sem, 1)

            def softmax_exp(i, step, n):
                act.wait_ge(d1_done.sem, d1_done.at(i, n + 1))
                s.activation(p1[:, n % 2], d1[:, n % 2], ACT.Exp).then_inc(p1_done.sem, 1)

            def body(i):
                for step in STEPS:
                    kind, n = step[0], step[1]
                    if kind == "xnT" and n % 2 == 0:
                        full(act, i, step)
                        copy(xnT[:, 0, :], tile(step)[:], xnT_act, step)
                    elif kind == "q":
                        full(act, i, step)
                        s.activation(qT[:, n, :], tile(step)[:], ACT.Identity,
                                     bias=bq4_col[:, n:n + 1], scale=QK).then_inc(free_of(step), 1)
                        act.drain().then_inc(q_done.sem, 1)
                    elif kind == "s2":
                        act.wait_ge(d2_done.sem, d2_done.at(i, 1))
                        s.activation(e2[:], d2[:], ACT.Exp, scale=1.0 / LSEG).then_inc(e2_done.sem, 1)
                    elif kind == "s3":
                        act.wait_ge(nm3_done.sem, nm3_done.at(i, n + 1))
                        if n >= 2:
                            full(act, i, ("p3T", n - 2))
                        s.activation(p3[:, n % 2], tile(step)[:], ACT.Exp, bias=nm3[:, n:n + 1],
                                     accum_out=sum3[:, n:n + 1]).then_inc(free_of(step), 1)
                        act.drain().then_inc(p3_done.sem, 1)
                    elif kind == "p3T":
                        full(act, i, step)
                        copy(p3T[:, n], tile(step)[:].rearrange("p (t c) -> p t c", t=T), p3T_done, step)
                    elif kind == "a":
                        full(act, i, step)
                        s.activation(uz[:, 4 * n:4 * n + 4, 0:LM],
                                     tile(step)[:, 0:256].rearrange("p (a b) -> p a b", a=4), ACT.Copy)
                        s.activation(ut[:, 4 * n:4 * n + 4, :],
                                     tile(step)[:, 256:512].rearrange("p (a b) -> p a b", a=4),
                                     ACT.Copy).then_inc(free_of(step), 1)
                        act.drain().then_inc(a_done.sem, 1)
                    elif kind == "s1":
                        if n >= 2:
                            full(act, i, ("p1T", n - 2))
                        else:
                            full_before(act, i, ("pxT", 6 + n))
                        softmax_exp(i, step, n)
                    elif kind == "p1T":
                        full(act, i, step)
                        if n == 0:
                            full_before(act, i, ("ox", 1))
                        copy(p1T[:, 4 * (n % 2):4 * (n % 2) + 4, (n // 2) * P:(n // 2 + 1) * P],
                             tile(step)[:].rearrange("p (a b) -> p a b", a=4), p1T_done, step)
                    elif kind == "qx":
                        full(act, i, step)
                        s.activation(qxT[:, n, :], tile(step)[:], ACT.Identity,
                                     bias=bqx_col[:, n:n + 1]).then_inc(free_of(step), 1)
                        act.drain().then_inc(qx_done.sem, 1)
                    elif kind == "sx":
                        full(act, i, ("pxT", n - 2) if n >= 2 else ("p1T", 6 + n))
                        softmax_exp(i, step, 8 + n)
                    elif kind == "pxT":
                        full(act, i, step)
                        if n == 0:
                            full(act, i, ("o1", 1))
                        copy(p1T[:, 4 * (n % 2):4 * (n % 2) + 4, (n // 2) * P:(n // 2 + 1) * P],
                             tile(step)[:].rearrange("p (a b) -> p a b", a=4), p1T_done, step)
                    elif kind == "gate":
                        full(act, i, step)
                        s.activation(gate_h[:], tile(step)[:, 0:1], ACT.Gelu,
                                     bias=bp1_col[:]).then_inc(free_of(step), 1)
                        act.drain().then_inc(gate_done.sem, 1)
                    elif kind == "logit":
                        act.wait_ge(sel_done.sem, sel_done.at(i, 1))
                        full_before(act, i, ("r", 1))
                        act.wait_ge(r_done.sem, r_done.before(i, 2))
                        act.sem_inc(act_turn, 1)
                        e = s.value_load(sel8[0:1, 0:1], min_val=0, max_val=7)
                        for dst, src in ((w1e[:], w1_dram[:, bass.ds(e * KD, KD), :]),
                                         (b1e[:], a["b1"][:, bass.ds(e * FM, FM)]),
                                         (w2e[:], w2_dram[:, bass.ds(e * FM, FM), :]),
                                         (b2e[:], a["b2"][:, bass.ds(e * KD, KD)])):
                            act.dma_start(dst, src).then_inc(expert_loaded.sem, 16)
                    elif kind == "h":
                        if n == 0:
                            act.wait_ge(expert_loaded.sem, expert_loaded.at(i, 64))
                        full(act, i, step)
                        s.activation(hT[:, n, :], tile(step)[:], ACT.Gelu,
                                     bias=b1e[:, n:n + 1]).then_inc(free_of(step), 1)
                        act.drain().then_inc(h_done.sem, 1)

            with act.Fori(0, B) as i:
                body(i)

        @block.vector
        def _(dve):
            v = nc.vector
            for sig in dve_makes:
                dve.sem_inc(sig.sem, sig.per)
            dve.wait_ge(consts_loaded, 16 * len(CONSTS))
            dve.wait_ge(pool_consts, 1)
            v.tensor_scalar(bq4_col[:], bqkv_col[:, 0:2], QK, None, ALU.mult)
            v.tensor_scalar(bfo3_row[:], bfo_row[:], 0.3, None, ALU.mult)
            v.drain().then_inc(dve_consts, 1)

            def normalise(i, n, src):
                for t in range(T):
                    v.bn_stats(stats[:, t, :], src[:, t, :])
                v.drain()
                for t in range(T):
                    v.bn_aggr(mv[:, t, :], stats[:, t, :])
                v.drain().then_inc(stats_done.sem, 1)
                dve.wait_ge(rstd_done.sem, rstd_done.at(i, n + 1))
                for t in range(T):
                    v.tensor_scalar(xn[:, t, :], src[:, t, :], mv[:, t, 0:1], rstd[:, t:t + 1],
                                    ALU.subtract, ALU.mult)
                v.drain().then_inc(xn_done.sem, 1)

            def copy(dst, src, sig, step):
                v.tensor_copy(dst, src).then_inc(free_of(step), 1)
                v.drain().then_inc(sig.sem, 1)

            def quarter(step, w):
                return tile(step)[:, 0:4 * w].rearrange("p (a b) -> p a b", a=4)

            def scores_down(i, step, n):
                full(dve, i, step)
                src = tile(step)[:].rearrange("p (h c) -> p h c", h=8)
                v.tensor_reduce(m1[:, n % 2], src, AX.X, ALU.max)
                v.drain()
                if n >= 2:
                    dve.wait_ge(p1_done.sem, p1_done.at(i, n - 1))
                else:
                    dve.wait_ge(p1_done.sem, p1_done.before(i, 15 + n))
                v.tensor_tensor(d1[:, n % 2], src, m1[:, n % 2].unsqueeze(2).broadcast_to([P, 8, LM]),
                                ALU.subtract).then_inc(free_of(step), 1)
                v.drain().then_inc(d1_done.sem, 1)

            def body(i):
                for step in STEPS:
                    kind, n = step[0], step[1]
                    if kind == "kx":
                        dve.wait_ge(ctx_loaded.sem, ctx_loaded.at(i, 32))
                        full_before(dve, i, ("sx", 7))
                        v.tensor_scalar(key_mask[:], mask_in[:], 0, None, ALU.not_equal)
                        v.tensor_scalar(neg_row[:], mask_in[0:3, :], 0, neg_col[:], ALU.is_equal, ALU.mult)
                        v.drain().then_inc(key_mask_done.sem, 1)
                        full(dve, i, step)
                        dve.wait_ge(kxbd_done.sem, kxbd_done.before(i, 1))
                        for k in range(KD):
                            last = v.scalar_tensor_tensor(kxT[:, k, :], tile(step)[:, k * LM:(k + 1) * LM],
                                                          bkx_col[:, k:k + 1], key_mask[:], ALU.add, ALU.mult)
                        last.then_inc(free_of(step), 1)
                        v.drain().then_inc(kx_done.sem, 1)
                    elif kind == "vx":
                        full(dve, i, step)
                        full_before(dve, i, ("ox", 1))
                        src = tile(step)[:, 0:D].rearrange("p (a h d) -> p a h d", a=PAIRS, h=2)
                        row = bvx_row[:].rearrange("p (a h d) -> p a h d", a=PAIRS, h=2)
                        for h in range(2):
                            q = slice(64 * h, 64 * h + 64)
                            last = v.tensor_tensor(vx_bd[q, :, DH * h:DH * h + DH], src[q, :, h], row[q, :, h],
                                                   ALU.add)
                        last.then_inc(free_of(step), 1)
                        v.drain().then_inc(vx_done.sem, 1)
                        dve.wait_ge(x_loaded.sem, x_loaded.at(i, 16))
                        normalise(i, 0, x_in)
                    elif kind == "xnT" and n % 2 == 1:
                        full(dve, i, step)
                        copy(xnT[:, 1, :], tile(step)[:], xnT_dve, step)
                    elif kind == "k":
                        full(dve, i, step)
                        v.tensor_scalar(kT[:, n, :], tile(step)[:], bqkv_col[:, 2 + n:3 + n], None,
                                        ALU.add).then_inc(free_of(step), 1)
                        v.drain().then_inc(k_done.sem, 1)
                        if n == 1:
                            dve.wait_ge(q_done.sem, q_done.at(i, 2))
                            for src, dst in ((qT, qsum), (kT, ksum)):
                                for k in range(KD):
                                    v.tensor_reduce(dst[:, k, :], src[:, k, :].rearrange(
                                        "p (m l) -> p m l", l=LSEG), AX.X, ALU.add)
                                v.drain().then_inc(lm_done.sem, 1)
                    elif kind == "v":
                        full(dve, i, step)
                        v.tensor_tensor(vt[:, 2 * n:2 * n + 2, :],
                                        tile(step)[:].rearrange("p (t d) -> p t d", t=2),
                                        bv_row[:].unsqueeze(1).broadcast_to([P, 2, D]),
                                        ALU.add).then_inc(free_of(step), 1)
                        v.drain().then_inc(v_done.sem, 1)
                    elif kind == "s2":
                        full(dve, i, step)
                        src = tile(step)[:].rearrange("p (a c) -> p a c", a=PAIRS)
                        v.tensor_reduce(m2[:], src, AX.X, ALU.max)
                        v.drain()
                        v.tensor_tensor(d2[:], src, m2[:].unsqueeze(2).broadcast_to([P, PAIRS, LM]),
                                        ALU.subtract).then_inc(free_of(step), 1)
                        v.drain().then_inc(d2_done.sem, 1)
                        dve.wait_ge(e2_done.sem, e2_done.at(i, 1))
                        v.tensor_reduce(r2[:], e2[:], AX.X, ALU.add)
                        v.drain()
                        v.reciprocal(r2[:], r2[:])
                        v.drain()
                        v.tensor_tensor(attn2[:], e2[:], r2[:].unsqueeze(2).broadcast_to([P, PAIRS, LM]),
                                        ALU.mult)
                        v.drain().then_inc(attn2_done.sem, 1)
                    elif kind == "x2T":
                        full(dve, i, step)
                        copy(attn2T[:], tile(step)[:].rearrange("p (a c) -> p a c", a=PAIRS),
                             attn2T_done, step)
                    elif kind == "s3":
                        full(dve, i, step)
                        v.tensor_reduce(nm3[:, n:n + 1], tile(step)[:], AX.X, ALU.max, negate=True)
                        v.drain().then_inc(nm3_done.sem, 1)
                    elif kind == "z":
                        full(dve, i, step)
                        dve.wait_ge(p3_done.sem, p3_done.at(i, PAIRS))
                        v.reciprocal(r3[:], sum3[:])
                        v.drain()
                        v.tensor_tensor(uz[:, :, LM:LM + DH],
                                        tile(step)[:, 0:P].rearrange("p (a d) -> p a d", a=PAIRS),
                                        r3[:].unsqueeze(2).broadcast_to([P, PAIRS, DH]),
                                        ALU.mult).then_inc(free_of(step), 1)
                        v.drain().then_inc(z_done.sem, 1)
                    elif kind in ("ps", "pe", "put", "puz"):
                        it, h = step[1:]
                        c = 3.25 ** -it
                        q = slice(4 * h, 4 * h + 4)
                        full(dve, i, step)
                        if kind == "ps":
                            v.scalar_tensor_tensor(dd[:, q, :], uz[:, q, 0:LM], -7.0 * c, quarter(step, LM),
                                                   ALU.mult, ALU.add).then_inc(free_of(step), 1)
                            v.drain().then_inc(dd_done.sem, 1)
                        elif kind == "pe":
                            v.scalar_tensor_tensor(gt[:, q, :], ut[:, q, :], 15.0 * c * c, quarter(step, LM),
                                                   ALU.mult, ALU.add).then_inc(free_of(step), 1)
                            v.drain().then_inc(gt_done.sem, 1)
                        elif kind == "put":
                            v.scalar_tensor_tensor(ut[:, q, :], quarter(step, LM), -1.0 / (13.0 * c ** 3),
                                                   ut[:, q, :], ALU.mult, ALU.add).then_inc(free_of(step), 1)
                            v.drain().then_inc(ut_done.sem, 1)
                        else:
                            lo = 0 if it < ITERS - 1 else LM
                            v.scalar_tensor_tensor(uz[:, q, lo:], quarter(step, LM + DH)[:, :, lo:],
                                                   -1.0 / (13.0 * c ** 3), uz[:, q, lo:],
                                                   ALU.mult, ALU.add).then_inc(free_of(step), 1)
                            v.drain().then_inc(uz_done.sem, 1)
                    elif kind == "y":
                        full(dve, i, step)
                        src = tile(step)[:, 0:P].rearrange("p (a d) -> p a d", a=PAIRS)
                        for h in range(2):
                            q = slice(64 * h, 64 * h + 64)
                            last = v.tensor_scalar(y_bd[q, :, DH * h:DH * h + DH], src[q], 3.25 ** ITERS,
                                                   None, ALU.mult)
                        last.then_inc(free_of(step), 1)
                        v.drain().then_inc(y_done.sem, 1)
                    elif kind == "s1":
                        scores_down(i, step, n)
                    elif kind == "sx":
                        scores_down(i, step, 8 + n)
                    elif kind in ("den1", "denx"):
                        full(dve, i, step)
                        v.reciprocal(rden[:, n, :], tile(step)[:]).then_inc(free_of(step), 1)
                        v.drain()
                    elif kind in ("o1", "ox"):
                        full(dve, i, step)
                        v.tensor_tensor(oT[:, n, :], tile(step)[:], rden[:, n, :],
                                        ALU.mult).then_inc(free_of(step), 1)
                        v.drain().then_inc(o_done.sem, 1)
                    elif kind in ("w1", "wx"):
                        full(dve, i, step)
                        dst, res, k, sig = (x1, xr, 1, x1_done) if kind == "w1" else (x2, x1b, 2, x2_done)
                        dve.wait_ge(xres_done.sem, xres_done.at(i, k))
                        if n == 0:
                            dve.wait_ge(xres_done.sem, xres_done.before(i, k + 1))
                        q = slice(2 * n, 2 * n + 2)
                        v.tensor_tensor(dst[:, q, :], tile(step)[:].rearrange("p (t d) -> p t d", t=2),
                                        res[:, q, :], ALU.add).then_inc(free_of(step), 1)
                        v.drain().then_inc(sig.sem, 1)
                        if n == 1:
                            normalise(i, k, dst)
                    elif kind == "logit":
                        full(dve, i, step)
                        v.tensor_tensor(logits[:], tile(step)[0:1, 0:8], bp2_row[:],
                                        ALU.add).then_inc(free_of(step), 1)
                        v.drain()
                        v.max(top8[:], logits[:])
                        v.drain()
                        v.max_index(sel8[:], top8[:], logits[:])
                        v.drain().then_inc(sel_done.sem, 1)
                    elif kind == "r":
                        full(dve, i, step)
                        dve.wait_ge(expert_loaded.sem, expert_loaded.at(i, 64))
                        v.tensor_scalar(rT[:, n, :], tile(step)[:], b2e[:, n:n + 1], None,
                                        ALU.add).then_inc(free_of(step), 1)
                        v.drain().then_inc(r_done.sem, 1)
                    elif kind == "y3":
                        full(dve, i, step)
                        dve.wait_ge(xres_done.sem, xres_done.at(i, 3))
                        dve.wait_ge(stored.sem, stored.before(i, 16))
                        q = slice(2 * n, 2 * n + 2)
                        v.scalar_tensor_tensor(yo[:, q, :], tile(step)[:].rearrange("p (t d) -> p t d", t=2),
                                               0.3, base2[:, q, :], ALU.mult, ALU.add)\
                            .then_inc(free_of(step), 1)
                        v.drain().then_inc(yo_done.sem, 1)

            with dve.Fori(0, B) as i:
                body(i)

        @block.tensor
        def _(pe):
            mm = nc.tensor.matmul
            pe.sem_inc(filled.sem, filled.per)
            pe.wait_ge(consts_loaded, 16 * len(CONSTS))
            pe.wait_ge(pool_consts, 1)

            def chain(dst, pairs):
                for k, (lhsT, rhs) in enumerate(pairs):
                    last = mm(dst, lhsT, rhs, start=(k == 0), stop=(k == len(pairs) - 1))
                return last

            def per_head(dst, lhsT, rhs, w, h):
                for x in range(4):
                    for r in range(2):
                        q = slice(64 * r, 64 * r + 64)
                        last = mm(dst[q, w * x:w * x + w], lhsT[q, 4 * h + x, 0:LM], rhs[q, 4 * h + x, 0:w],
                                  start=True, stop=True)
                return last

            def tokens(n):
                return n // 2, n % 2, slice((n // 2) * P, (n // 2 + 1) * P)

            def body(i):
                for step in STEPS:
                    kind, n = step[0], step[1]
                    o = tile(step)
                    b, turn = FILL[step] % BANKS, FILL[step] // BANKS
                    pe.wait_ge(free[b].sem, free[b].at(i, turn))
                    if kind == "kx":
                        pe.wait_ge(ctx_loaded.sem, ctx_loaded.at(i, 32))
                        for m in range(KD):
                            last = chain(o[:, m * LM:(m + 1) * LM],
                                         [(wk[:, k, m * P:(m + 1) * P], ctxT[:, k, :]) for k in range(KD)])
                    elif kind == "vx":
                        for r in range(2):
                            last = chain(o[64 * r:64 * r + 64, 0:D],
                                         [(ctxT[:, k, :], wv[:, k, :]) for k in range(KD)])
                    elif kind == "xnT":
                        pe.wait_ge(xn_done.sem, xn_done.at(i, n // 2 + 1))
                        for t in range(T):
                            last = nc.tensor.transpose(o[:, t * P:(t + 1) * P],
                                                       xn[:, t, (n % 2) * P:(n % 2 + 1) * P], ident[:])
                    elif kind in ("q", "k"):
                        if step == ("q", 0):
                            pe.wait_ge(xnT_act.sem, xnT_act.at(i, 1))
                            pe.wait_ge(xnT_dve.sem, xnT_dve.at(i, 1))
                        c = (n + 2 * (kind == "k")) * P
                        last = chain(o[:], [(wqkv[:, k, c:c + P], xnT[:, k, :]) for k in range(KD)])
                    elif kind == "v":
                        for t in range(2):
                            q = slice((2 * n + t) * P, (2 * n + t + 1) * P)
                            last = chain(o[:, t * D:(t + 1) * D],
                                         [(xnT[:, k, q], wqkv[:, k, 2 * D:3 * D]) for k in range(KD)])
                    elif kind == "s2":
                        pe.wait_ge(bd_done.sem, bd_done.at(i, 2))
                        for x in range(PAIRS):
                            last = mm(o[:, x * LM:(x + 1) * LM], pair_of(qbd, x), ksum[:, x // 4, :],
                                      start=True, stop=True)
                    elif kind == "s3":
                        last = mm(o[:], pair_of(qbd, n), kT[:, n // 4, :], start=True, stop=True)
                    elif kind == "x2T":
                        pe.wait_ge(attn2_done.sem, attn2_done.at(i, 1))
                        pe.sem_inc(pe_turn, 1)
                        for x in range(PAIRS):
                            for r in range(2):
                                q = slice(64 * r, 64 * r + 64)
                                last = mm(o[q, x * LM:(x + 1) * LM], attn2[q, x, :], ident[q, q],
                                          start=True, stop=True)
                    elif kind == "p3T":
                        pe.wait_ge(p3_done.sem, p3_done.at(i, n + 1))
                        for t in range(T):
                            last = nc.tensor.transpose(o[:, t * P:(t + 1) * P],
                                                       p3[:, n % 2, t * P:(t + 1) * P], ident[:])
                    elif kind == "a":
                        if n == 0:
                            pe.wait_ge(attn2T_done.sem, attn2T_done.at(i, 1))
                        pe.sem_inc(pe_turn, 1)
                        per_head(o, attn2T, attn2, LM, n)
                        last = per_head(o[:, 256:512], attn2, attn2T, LM, n)
                    elif kind == "z":
                        pe.wait_ge(p3T_done.sem, p3T_done.at(i, PAIRS))
                        pe.wait_ge(v_done.sem, v_done.at(i, 2))
                        for x in range(PAIRS):
                            for r in range(2):
                                c = (2 * x + r) * DH
                                last = chain(o[64 * r:64 * r + 64, x * DH:(x + 1) * DH],
                                             [(p3T[:, x, t, 64 * r:64 * r + 64], vt[:, t, c:c + DH])
                                              for t in range(T)])
                    elif kind == "ps":
                        it, h = step[1:]
                        if it == 0:
                            pe.wait_ge(a_done.sem, a_done.at(i, h + 1))
                            if h == 0:
                                pe.wait_ge(z_done.sem, z_done.at(i, 1))
                        else:
                            pe.wait_ge(uz_done.sem, uz_done.at(i, 2 * (it - 1) + h + 1))
                            pe.wait_ge(ut_done.sem, ut_done.at(i, 2 * (it - 1) + h + 1))
                        pe.sem_inc(pe_turn, 1)
                        last = per_head(o, ut, uz, LM, h)
                    elif kind == "pe":
                        it, h = step[1:]
                        pe.wait_ge(dd_done.sem, dd_done.at(i, 2 * it + h + 1))
                        pe.sem_inc(pe_turn, 1)
                        last = per_head(o, dd, ut, LM, h)
                    elif kind == "put":
                        it, h = step[1:]
                        pe.wait_ge(gt_done.sem, gt_done.at(i, 2 * it + h + 1))
                        pe.sem_inc(pe_turn, 1)
                        last = per_head(o, uz, gt, LM, h)
                    elif kind == "puz":
                        it, h = step[1:]
                        pe.wait_ge(gt_done.sem, gt_done.at(i, 2 * it + h + 1))
                        pe.sem_inc(pe_turn, 1)
                        w = LM + DH
                        if it < ITERS - 1:
                            last = per_head(o, gt, uz, w, h)
                        else:
                            for x in range(4):
                                for r in range(2):
                                    q = slice(64 * r, 64 * r + 64)
                                    last = mm(o[q, w * x + LM:w * x + w], gt[q, 4 * h + x, :],
                                              uz[q, 4 * h + x, LM:w], start=True, stop=True)
                    elif kind == "y":
                        pe.wait_ge(uz_done.sem, uz_done.at(i, 2 * ITERS))
                        pe.sem_inc(pe_turn, 1)
                        for x in range(PAIRS):
                            for r in range(2):
                                q = slice(64 * r, 64 * r + 64)
                                last = mm(o[q, x * DH:(x + 1) * DH], attn2T[q, x, :], uz[q, x, LM:LM + DH],
                                          start=True, stop=True)
                    elif kind == "s1":
                        t, k, q = tokens(n)
                        last = mm(o[:], qT[:, k, q], kbd[:, k].rearrange("p h c -> p (h c)"),
                                  start=True, stop=True)
                    elif kind in ("p1T", "pxT"):
                        m = n + 8 * (kind == "pxT")
                        pe.wait_ge(p1_done.sem, p1_done.at(i, m + 1))
                        for x in range(4):
                            last = nc.tensor.transpose(o[:, x * P:(x + 1) * P], p1[:, m % 2, x, :], ident[:])
                    elif kind in ("den1", "denx", "o1", "ox"):
                        first = kind in ("den1", "o1")
                        if kind[0] == "d" and n == 0:
                            pe.wait_ge(p1T_done.sem, p1T_done.at(i, 8 if first else 16))
                            if first:
                                pe.wait_ge(y_done.sem, y_done.at(i, 1))
                            else:
                                pe.wait_ge(vx_done.sem, vx_done.at(i, 1))
                        for x in range(4):
                            if kind[0] == "d":
                                w = ones_bd[:]
                            else:
                                w = (y_bd if first else vx_bd)[:, 4 * n + x, :]
                            last = mm(o[32 * x:32 * x + 32, :], w, p1T[:, 4 * n + x, :], start=True, stop=True)
                    elif kind in ("w1", "wx"):
                        if n == 0:
                            pe.wait_ge(o_done.sem, o_done.at(i, 2 if kind == "w1" else 4))
                        for t in range(2):
                            q = slice((2 * n + t) * P, (2 * n + t + 1) * P)
                            w = wout if kind == "w1" else wo
                            last = chain(o[:, t * D:(t + 1) * D],
                                         [(oT[:, k, q], w[:, k, :]) for k in range(KD)])
                    elif kind == "qx":
                        if n == 0:
                            pe.wait_ge(xnT_act.sem, xnT_act.at(i, 2))
                            pe.wait_ge(xnT_dve.sem, xnT_dve.at(i, 2))
                        last = chain(o[:], [(wq[:, k, n * P:(n + 1) * P], xnT[:, k, :]) for k in range(KD)])
                    elif kind == "sx":
                        t, k, q = tokens(n)
                        if n == 0:
                            pe.wait_ge(qx_done.sem, qx_done.at(i, 2))
                            pe.wait_ge(kxbd_done.sem, kxbd_done.at(i, 1))
                        mm(o[:], qxT[:, k, q], kx_bd[:, k].rearrange("p h c -> p (h c)"),
                           start=True, stop=False)
                        last = mm(o[:], ones3[:], neg_row[:].unsqueeze(1).broadcast_to([3, 8, LM]),
                                  start=False, stop=True)
                    elif kind == "gate":
                        pe.wait_ge(xnT_act.sem, xnT_act.at(i, 3))
                        pe.wait_ge(xnT_dve.sem, xnT_dve.at(i, 3))
                        last = chain(o[:, 0:1], [(wp1[:, k, :], xnT[:, k, S - 1:S]) for k in range(KD)])
                    elif kind == "logit":
                        pe.wait_ge(gate_done.sem, gate_done.at(i, 1))
                        last = mm(o[0:1, 0:8], gate_h[:], wp2[:], start=True, stop=True)
                    elif kind == "h":
                        if n == 0:
                            pe.wait_ge(expert_loaded.sem, expert_loaded.at(i, 64))
                        last = chain(o[:], [(w1e[:, k, n * P:(n + 1) * P], xnT[:, k, :]) for k in range(KD)])
                    elif kind == "r":
                        if n == 0:
                            pe.wait_ge(h_done.sem, h_done.at(i, FM))
                        last = chain(o[:], [(w2e[:, k, n * P:(n + 1) * P], hT[:, k, :]) for k in range(FM)])
                    elif kind == "y3":
                        if n == 0:
                            pe.wait_ge(r_done.sem, r_done.at(i, 2))
                        for t in range(2):
                            q = slice((2 * n + t) * P, (2 * n + t + 1) * P)
                            last = chain(o[:, t * D:(t + 1) * D],
                                         [(rT[:, k, q], wfo[:, k, :]) for k in range(KD)])
                    last.then_inc(filled.sem, 1)

            def pair_of(t, x):
                return t[:, x // 4, 2 * (x % 4):2 * (x % 4) + 2, :].rearrange("p h c -> p (h c)")

            with pe.Fori(0, B) as i:
                body(i)


def kernel(**inputs):
    import numpy as _np
    import concourse.bacc as _bacc
    from concourse import mybir as _mybir
    from concourse.bass_utils import run_bass_kernel_spmd as _run

    def get(name):
        return _np.asarray(inputs[name])

    def cols(v):
        v = v.reshape(-1, 128)
        return v.T

    def rows(v):
        return _np.broadcast_to(v[None, :], (128, v.shape[0]))

    layout = {
        "x": get("x"),
        "ctxT": get("ctx_1024").transpose(0, 2, 1),
        "mask": rows(get("mask_Bx1x1xS2_ik0").reshape(-1)),
        "Wqkv": get("L0_attn_Wqkv"),
        "bqkv": cols(get("L0_attn_bqkv")),
        "bv": rows(get("L0_attn_bqkv")[512:768]),
        "Wout": get("L0_attn_Wout"),
        "bout": rows(get("L0_attn_bout")),
        "WqT": get("L0_xattn_Wq").T,
        "bqx": cols(get("L0_xattn_bq")),
        "WkT": get("L0_xattn_Wk").T,
        "bkx": cols(get("L0_xattn_bk")),
        "WvT": get("L0_xattn_Wv").T,
        "bvx": rows(get("L0_xattn_bv")),
        "WoT": get("L0_xattn_Wo").T,
        "box": rows(get("L0_xattn_bo")),
        "Wp1": get("L0_ffn_Wp1"),
        "bp1": cols(get("L0_ffn_bp1")),
        "Wp2": get("L0_ffn_Wp2"),
        "bp2": get("L0_ffn_bp2")[None, :],
        "W1": get("L0_ffn_W1"),
        "b1": cols(get("L0_ffn_b1")),
        "W2": get("L0_ffn_W2"),
        "b2": cols(get("L0_ffn_b2")),
        "Wfo": get("L0_ffn_Wo"),
        "bfo": rows(get("L0_ffn_bo")),
    }
    nc = _bacc.Bacc("TRN2", target_bir_lowering=False, num_devices=1)
    arrays, aps = {}, {}
    for name, arr in layout.items():
        arr = _np.ascontiguousarray(arr)
        arrays[f"in_{name}"] = arr
        aps[name] = nc.dram_tensor(f"in_{name}", arr.shape, _mybir.dt.from_np(arr.dtype),
                                   kind="ExternalInput").ap()
    out = nc.dram_tensor("out_0", get("x").shape, _mybir.dt.float32, kind="ExternalOutput").ap()
    decoder_kernel(nc, aps, out)
    r = _run(nc, [arrays], core_ids=[0])
    return r.results[0]["out_0"]
```

```python
from contextlib import ExitStack

import concourse.bass as bass
from concourse import mybir

ALU = mybir.AluOpType
ACT = mybir.ActivationFunctionType
AX = mybir.AxisListType
F32 = mybir.dt.float32
BF16 = mybir.dt.bfloat16
I32 = mybir.dt.int32
U32 = mybir.dt.uint32

P = 128
HEADS = 16
DH = 16
LM = 64
PAIRS = HEADS // 2
ITERS = 6
BANKS = 8
SLOTS = 3
EPS = 1e-5
NEG_PARTS = (-998244352.0, -1753088.0, -2560.0)
assert sum(NEG_PARTS) == -1e9


def attention_steps():
    s = [("lnA", 0), ("xnTa", 0), ("xnTa", 1)]
    s += [("q", 0), ("q", 1), ("k", 0), ("k", 1), ("v", 0), ("v", 1)]
    s += [("s3", 0), ("s3", 1), ("s2", 0), ("p3T", 0), ("s3", 2), ("p3T", 1)]
    s += [("s3", 3), ("p3T", 2), ("s3", 4), ("p3T", 3), ("x2T", 0), ("s3", 5), ("p3T", 4)]
    s += [("s3", 6), ("p3T", 5), ("a", 0), ("a", 1), ("s3", 7), ("p3T", 6), ("p3T", 7)]
    s += [("zT", 0), ("zT", 1), ("z", 0)]
    fillers = []
    for n in range(8):
        fillers.append(("s1", n))
        if n >= 1:
            fillers.append(("p1T", n - 1))
    fillers += [("p1T", 7), ("den1", 0), ("den1", 1)]
    for it in range(ITERS):
        for part in ("ps", "pe"):
            s += [(part, it, 0), (part, it, 1)]
            if fillers:
                s.append(fillers.pop(0))
        for h in range(2):
            if it < ITERS - 1:
                s.append(("put", it, h))
            s.append(("puz", it, h))
            if fillers:
                s.append(fillers.pop(0))
    s += [("y", 0)]
    s += fillers
    s += [("o1", 0), ("o1", 1), ("w1", 0), ("w1", 1)]
    return s


def rest_steps():
    s = [("kx", 0), ("vx", 0), ("lnB", 0), ("xnTb", 0), ("xnTb", 1), ("qx", 0), ("qx", 1)]
    for n in range(8):
        s.append(("sx", n))
        if n >= 1:
            s.append(("pxT", n - 1))
    s += [("pxT", 7)]
    s += [("denx", 0), ("denx", 1), ("ox", 0), ("ox", 1), ("wx", 0), ("wx", 1)]
    s += [("lnB", 1), ("xnTb", 2), ("xnTb", 3), ("gate", 0), ("logit", 0)]
    return s


def expert_steps():
    s = [("h", m) for m in range(4)] + [("r", 0), ("r", 1), ("y3", 0), ("y3", 1)]
    return s


STEP_US = {
    "lnA": 0, "xnTa": 0.5, "q": 1.7, "k": 1.7, "v": 1.7, "s2": 1.7, "s3": 0.9, "x2T": 1.2,
    "p3T": 0.5, "a": 1.2, "zT": 0.9, "z": 0.4, "ps": 0.6, "pe": 0.6, "put": 0.6, "puz": 0.7,
    "y": 1.2, "s1": 0.9, "p1T": 0.5, "den1": 0.9, "o1": 0.9, "w1": 1.7,
    "kx": 0.9, "vx": 0.9, "lnB": 0, "xnTb": 0.5, "qx": 1.7, "sx": 1.1, "pxT": 0.5, "denx": 0.9,
    "ox": 0.9, "wx": 1.7, "gate": 0.4, "logit": 0.3, "h": 1.7, "r": 3.4, "y3": 1.7,
}
LEAD_US = {("xnTa", 0): 5, ("q", 0): 1, ("s3", 0): 2, ("s2", 0): 1, ("z", 0): 1, ("y", 0): 1, ("w1", 0): 6,
           ("xnTb", 0): 4, ("qx", 0): 1, ("denx", 0): 2, ("wx", 0): 5, ("lnB", 1): 1, ("xnTb", 2): 10,
           ("gate", 0): 2, ("logit", 0): 2, "experts": 12}


def interleave(*streams):
    timed = []
    for x, steps in enumerate(streams):
        now, starts = 0.0, []
        for step in steps:
            now += LEAD_US.get(step, 0)
            starts.append(starts[-1] if step[0] == "h" and step[1] else now)
            now += STEP_US[step[0]]
        if step == ("logit", 0):
            now += LEAD_US["experts"]
        timed += [(t / now, x, n, step) for n, (t, step) in enumerate(zip(starts, steps))]
    return [t[3] for t in sorted(timed)]


A_STEPS, B_STEPS, E_STEPS = attention_steps(), rest_steps(), expert_steps()
AB_STEPS = interleave(A_STEPS, B_STEPS)
AEB_STEPS = interleave(A_STEPS, E_STEPS + B_STEPS)
A_BANKS, B_BANKS = (0, 1, 2, 3), (4, 5, 6, 7)
IN_B, IN_E = {*B_STEPS, *E_STEPS}, set(E_STEPS)
FILL, BANK, TURN, USES = {}, {}, {}, [0] * BANKS
for _steps, _banks in ((A_STEPS, A_BANKS), (B_STEPS + E_STEPS, B_BANKS)):
    for _n, _step in enumerate(x for x in _steps if x[0] not in ("lnA", "lnB")):
        FILL[_step] = _n
        BANK[_step] = _banks[_n % len(_banks)]
        TURN[_step] = _n // len(_banks)
        USES[BANK[_step]] += 1


class Signal:

    def __init__(self, sem, per):
        self.sem, self.per = sem, per

    def at(self, i, k):
        return (i + 1) * self.per + k

    def before(self, i, k):
        return i * self.per + k


def decoder_kernel(nc, a, out):
    B, S, D = a["x"].shape
    T = S // P
    KD = D // P
    FF = 512
    FM = FF // P
    LSEG = S // LM
    QK = 0.25

    with ExitStack() as ctx:
        def sb(name, shape, dt=F32):
            return ctx.enter_context(nc.sbuf_tensor(name, shape, dt))

        def sem(name):
            return ctx.enter_context(nc.semaphore(name))

        bank = [ctx.enter_context(nc.psum_tensor(f"bank{b}", [P, 512], F32)) for b in range(BANKS)]

        wqkv = sb("wqkv", [P, KD, 3 * D])
        wout = sb("wout", [P, KD, D])
        wq = sb("wq", [P, KD, D])
        wk = sb("wk", [P, KD, D])
        wv = sb("wv", [P, KD, D])
        wo = sb("wo", [P, KD, D])
        wp1 = sb("wp1", [P, KD, P])
        wp2 = sb("wp2", [P, 8])
        wfo = sb("wfo", [P, KD, D])
        bqkv_col = sb("bqkv_col", [P, 6])
        bq4_col = sb("bq4_col", [P, 2])
        bqx_col = sb("bqx_col", [P, 2])
        bkx_col = sb("bkx_col", [P, 2])
        bp1_col = sb("bp1_col", [P, 1])
        bp2_row = sb("bp2_row", [1, 8])
        bv_row = sb("bv_row", [P, D])
        bout_row = sb("bout_row", [P, D])
        bvx_row = sb("bvx_row", [P, D])
        box_row = sb("box_row", [P, D])
        bfo_row = sb("bfo_row", [P, D])
        bfo3_row = sb("bfo3_row", [P, D])
        ident = sb("ident", [P, P])
        head_mask = sb("head_mask", [P, 8])
        head_mean = sb("head_mean", [P, 8])
        ones_bd = sb("ones_bd", [P, 32])
        ones3 = sb("ones3", [3, P], BF16)
        neg_col = sb("neg_col", [3, 1])
        x_in = sb("x_in", [P, T, D])
        xr = sb("xr", [P, T, D])
        stats = {x: sb(f"stats_{x}", [P, T, 6]) for x in "ab"}
        mv = {x: sb(f"mv_{x}", [P, T, 2]) for x in "ab"}
        var_eps = {x: sb(f"var_eps_{x}", [P, T]) for x in "ab"}
        rstd = {x: sb(f"rstd_{x}", [P, T]) for x in "ab"}
        xo = {x: sb(f"xo_{x}", [P, T * D]) for x in "ab"}
        xn = {x: xo[x][:].rearrange("p (t d) -> p t d", t=T) for x in "ab"}
        oT = {x: xo[x][:].rearrange("p (k s) -> p k s", k=KD) for x in "ab"}
        xnT = {x: sb(f"xnT_{x}", [P, KD, S]) for x in "ab"}
        m1 = {x: sb(f"m1_{x}", [P, SLOTS, 8]) for x in "ab"}
        p1 = {x: sb(f"p1_{x}", [P, SLOTS, 8, LM]) for x in "ab"}
        p1T = {x: sb(f"p1T_{x}", [P, PAIRS, S]) for x in "ab"}
        rden = {x: sb(f"rden_{x}", [P, 2, S]) for x in "ab"}
        minus_half = sb("minus_half", [P, T])
        qT = sb("qT", [P, KD, S])
        kT = sb("kT", [P, KD, S])
        vt = sb("vt", [P, T, D])
        qsum = sb("qsum", [P, KD, LM])
        ksum = sb("ksum", [P, KD, LM])
        qbd = sb("qbd", [P, KD, 8, LM])
        kbd = sb("kbd", [P, KD, 8, LM])
        m2 = sb("m2", [P, PAIRS])
        r2 = sb("r2", [P, PAIRS])
        attn2 = sb("attn2", [P, PAIRS, LM])
        attn2T = sb("attn2T", [P, PAIRS, LM])
        nm3 = sb("nm3", [P, PAIRS])
        sum3 = sb("sum3", [P, PAIRS])
        r3 = sb("r3", [P, PAIRS])
        zT = sb("zT", [P, 2, P])
        p3 = sb("p3", [P, 2, S])
        p3T = p1T["a"][:].rearrange("p a (t c) -> p a t c", t=T)
        uz = sb("uz", [P, PAIRS, LM + DH])
        ut = sb("ut", [P, PAIRS, LM])
        dd = sb("dd", [P, PAIRS, LM])
        gt = sb("gt", [P, PAIRS, LM])
        y_bd = sb("y_bd", [P, PAIRS, 32])
        x1 = sb("x1", [P, T, D])
        x1b = sb("x1b", [P, T, D])
        ctxT = sb("ctxT", [P, KD, LM])
        mask_in = sb("mask_in", [P, LM], I32)
        key_mask = sb("key_mask", [P, LM])
        neg_row = sb("neg_row", [3, LM], BF16)
        kxT = sb("kxT", [P, KD, LM])
        kx_bd = sb("kx_bd", [P, KD, 8, LM])
        vx_bd = sb("vx_bd", [P, PAIRS, 32])
        qxT = sb("qxT", [P, KD, S])
        x2 = sb("x2", [P, T, D])
        base = sb("base", [P, T, D])
        gate_h = sb("gate_h", [P, 1])
        logits = sb("logits", [1, 8])
        top8 = sb("top8", [1, 8])
        sel8 = sb("sel8", [1, 8], U32)
        w1e = sb("w1e", [P, KD, FF])
        w2e = sb("w2e", [P, FM, D])
        b1e = sb("b1e", [P, FM])
        b2e = sb("b2e", [P, KD])
        hT = sb("hT", [P, FM, S])
        rT = qxT
        yo = sb("yo", [P, T, D])

        filled = {"a": Signal(sem("a_tiles_filled"), sum(x not in IN_B for x in FILL)),
                  "b": Signal(sem("b_tiles_filled"), sum(x in IN_B for x in FILL))}
        taken = [Signal(sem(f"bank{b}_taken"), USES[b]) for b in range(BANKS)]
        consts_loaded = sem("consts_loaded")
        x_loaded = Signal(sem("x_loaded"), 16)
        ctx_loaded = Signal(sem("ctx_loaded"), 32)
        expert_loaded = Signal(sem("expert_loaded"), 64)
        stored = Signal(sem("stored"), 16)
        pool_consts = sem("pool_consts")
        dve_consts = sem("dve_consts")
        stats_done = {"a": Signal(sem("a_stats_done"), 1), "b": Signal(sem("b_stats_done"), 2)}
        rstd_done = {"a": Signal(sem("a_rstd_done"), 1), "b": Signal(sem("b_rstd_done"), 2)}
        xn_done = {"a": Signal(sem("a_xn_done"), 1), "b": Signal(sem("b_xn_done"), 2)}
        p1_done = {"a": Signal(sem("a_p1_done"), 8), "b": Signal(sem("b_p1_done"), 8)}
        lm_done = Signal(sem("lm_done"), 2)
        bd_done = Signal(sem("bd_done"), 4)
        e2_done = Signal(sem("e2_done"), 1)
        attn2_done = Signal(sem("attn2_done"), 1)
        nm3_done = Signal(sem("nm3_done"), PAIRS)
        xr_done = Signal(sem("xr_done"), 1)
        x1b_done = Signal(sem("x1b_done"), 1)
        base_done = Signal(sem("base_done"), 1)
        key_mask_done = Signal(sem("key_mask_done"), 1)
        kxbd_done = Signal(sem("kxbd_done"), 1)
        sel_done = Signal(sem("sel_done"), 1)
        pe_turn, act_turn = sem("pe_turn"), sem("act_turn")
        pool_turn, sp_turn = sem("pool_turn"), sem("sp_turn")

        dve_makes = [*stats_done.values(), *xn_done.values(), lm_done, attn2_done, nm3_done,
                     key_mask_done, sel_done, *taken]
        act_makes = [*p1_done.values(), e2_done, expert_loaded]
        pool_makes = [*rstd_done.values(), bd_done, xr_done, x1b_done, base_done, kxbd_done]

        def stream(step):
            return "b" if step in IN_B else "a"

        def tile(step):
            return bank[BANK[step]]

        def done(ins, step):
            return ins.then_inc(taken[BANK[step]].sem, 1)

        def full(eng, i, step):
            f = filled[stream(step)]
            eng.wait_ge(f.sem, f.at(i, FILL[step] + 1))

        def full_before(eng, i, step):
            f = filled[stream(step)]
            eng.wait_ge(f.sem, f.before(i, FILL[step] + 1))

        def read(eng, i, *steps):
            for b in sorted({BANK[s] for s in steps}):
                turn = max(TURN[s] for s in steps if BANK[s] == b)
                eng.wait_ge(taken[b].sem, taken[b].at(i, turn + 1))

        def read_before(eng, i, step):
            f = taken[BANK[step]]
            eng.wait_ge(f.sem, f.before(i, TURN[step] + 1))

        def run(eng, body):
            def turn(steps, row_a, row_b, row_e):
                for step in steps:
                    body(row_e if step in IN_E else row_b if step in IN_B else row_a, step)

            turn(A_STEPS, 0, None, None)
            turn(AB_STEPS, 1, 0, None)
            with eng.Fori(2, B) as i:
                turn(AEB_STEPS, i, i - 1, i - 2)
            turn(E_STEPS + B_STEPS, None, B - 1, B - 2)
            turn(E_STEPS, None, None, B - 1)

        block = ctx.enter_context(nc.Block())
        x_dram = a["x"].rearrange("b (t p) d -> p (b t) d", p=P)
        out_dram = out.rearrange("b (t p) d -> p (b t) d", p=P)
        ctx_dram = a["ctxT"].rearrange("b (k p) c -> p (b k) c", p=P)
        mask_dram = a["mask"]
        w1_dram = a["W1"].rearrange("e (k p) f -> p (e k) f", p=P)
        w2_dram = a["W2"].rearrange("e (k p) f -> p (e k) f", p=P)

        def halves(w):
            return w.rearrange("(k p) n -> p k n", p=P)

        CONSTS = [
            (wqkv[:], halves(a["Wqkv"])), (bqkv_col[:], a["bqkv"]), (bv_row[:], a["bv"]),
            (wk[:], halves(a["WkT"])), (wv[:], halves(a["WvT"])), (bkx_col[:], a["bkx"]),
            (bvx_row[:], a["bvx"]), (wout[:], halves(a["Wout"])), (bout_row[:], a["bout"]),
            (wq[:], halves(a["WqT"])), (bqx_col[:], a["bqx"]), (wo[:], halves(a["WoT"])),
            (box_row[:], a["box"]), (wp1[:], halves(a["Wp1"])), (bp1_col[:], a["bp1"]),
            (wp2[:], a["Wp2"]), (bp2_row[:], a["bp2"]), (wfo[:], halves(a["Wfo"])),
            (bfo_row[:], a["bfo"]),
        ]

        @block.sync
        def _(sp):
            def load_x(i, first=False):
                if not first:
                    sp.wait_ge(xn_done["a"].sem, xn_done["a"].before(i, 1))
                    sp.sem_inc(sp_turn, 1)
                    sp.wait_ge(xr_done.sem, xr_done.before(i, 1))
                    sp.sem_inc(sp_turn, 1)
                sp.dma_start(x_in[:], x_dram[:, bass.ds(i * T, T), :]).then_inc(x_loaded.sem, 16)

            def load_context(i, first=False):
                if not first:
                    full_before(sp, i, ("vx", 0))
                    sp.sem_inc(sp_turn, 1)
                    sp.wait_ge(key_mask_done.sem, key_mask_done.before(i, 1))
                    sp.sem_inc(sp_turn, 1)
                sp.dma_start(ctxT[:], ctx_dram[:, bass.ds(i * KD, KD), :]).then_inc(ctx_loaded.sem, 16)
                sp.dma_start(mask_in[:], mask_dram[:, bass.ds(i * LM, LM)]).then_inc(ctx_loaded.sem, 16)

            def store(i):
                read(sp, i, ("y3", 0))
                sp.sem_inc(sp_turn, 1)
                read(sp, i, ("y3", 1))
                sp.sem_inc(sp_turn, 1)
                sp.dma_start(out_dram[:, bass.ds(i * T, T), :], yo[:]).then_inc(stored.sem, 16)

            sp.sem_inc(x_loaded.sem, 16)
            sp.sem_inc(ctx_loaded.sem, 32)
            sp.sem_inc(stored.sem, 16)
            load_x(0, first=True)
            for dst, src in CONSTS:
                sp.dma_start(dst, src).then_inc(consts_loaded, 16)
            load_context(0, first=True)
            load_x(1)
            load_x(2)
            with sp.Fori(2, B - 1) as i:
                load_context(i - 1)
                load_x(i + 1)
                store(i - 2)
            load_context(B - 2)
            store(B - 3)
            load_context(B - 1)
            store(B - 2)
            store(B - 1)
            sp.wait_ge(stored.sem, stored.at(B - 1, 16))

        @block.gpsimd
        def _(pool):
            g = nc.gpsimd
            for s in pool_makes:
                pool.sem_inc(s.sem, s.per)
            g.memset(ident[:], 0.0)
            g.memset(head_mask[:], 1.0)
            g.memset(ones_bd[:], 0.0)
            g.memset(neg_col[:], NEG_PARTS[0])
            g.memset(y_bd[:], 0.0)
            g.memset(vx_bd[:], 0.0)
            g.memset(ones3[:], 1.0)
            g.memset(minus_half[:], -0.5)
            g.drain()
            g.affine_select(out=ident[:], in_=ident[:], compare_op=ALU.not_equal, fill=1.0,
                            base=0, pattern=[[-1, P]], channel_multiplier=1)
            g.affine_select(out=head_mask[:], in_=head_mask[:], compare_op=ALU.is_ge, fill=0.0,
                            base=0, pattern=[[-DH, 8]], channel_multiplier=1)
            g.drain()
            g.memset(ones_bd[0:64, 0:16], 1.0)
            g.drain()
            g.memset(ones_bd[64:128, 16:32], 1.0)
            g.drain()
            g.affine_select(out=neg_col[:], in_=neg_col[:], compare_op=ALU.not_equal,
                            fill=NEG_PARTS[1], base=-1, pattern=[[0, 1]], channel_multiplier=1)
            g.drain()
            g.affine_select(out=head_mask[:], in_=head_mask[:], compare_op=ALU.is_ge, fill=0.0,
                            base=DH - 1, pattern=[[DH, 8]], channel_multiplier=-1)
            g.affine_select(out=neg_col[:], in_=neg_col[:], compare_op=ALU.not_equal,
                            fill=NEG_PARTS[2], base=-2, pattern=[[0, 1]], channel_multiplier=1)
            g.drain()
            g.tensor_scalar(head_mean[:], head_mask[:], 1.0 / LSEG, None, ALU.mult)
            g.tensor_scalar(head_mask[:], head_mask[:], QK, None, ALU.mult)
            g.drain().then_inc(pool_consts, 1)
            pool.wait_ge(consts_loaded, 16 * len(CONSTS))
            pool.wait_ge(dve_consts, 1)

            def layer_rstd(i, x, n):
                pool.wait_ge(stats_done[x].sem, stats_done[x].at(i, n + 1))
                pool.sem_inc(pool_turn, 1)
                g.tensor_scalar(var_eps[x][:], mv[x][:, :, 1], EPS, None, ALU.add)
                g.drain()
                g.tensor_tensor(rstd[x][:], var_eps[x][:], minus_half[:], ALU.pow)\
                    .then_inc(rstd_done[x].sem, 1)

            def spread(dst, src, scale):
                return g.tensor_tensor(dst, src.unsqueeze(1).broadcast_to([P, 8, LM]),
                                       scale.unsqueeze(2).broadcast_to([P, 8, LM]), ALU.mult)

            def add_row(dst, src, row):
                return g.tensor_tensor(dst, src, row[:].unsqueeze(1).broadcast_to([P, T, D]), ALU.add)

            def body(i, step):
                if step == ("kx", 0):
                    read(pool, i, step)
                    full_before(pool, i, ("sx", 7))
                    for k in range(KD):
                        last = spread(kx_bd[:, k], kxT[:, k], head_mask[:])
                    last.then_inc(kxbd_done.sem, 1)
                elif step == ("lnA", 0):
                    layer_rstd(i, "a", 0)
                    pool.wait_ge(x_loaded.sem, x_loaded.at(i, 16))
                    read_before(pool, i, ("w1", 1))
                    add_row(xr[:], x_in[:], bout_row).then_inc(xr_done.sem, 1)
                elif step == ("q", 1) or step == ("k", 1):
                    full_before(pool, i, ("s1", 7))
                    dst, src, n = (qbd, qsum, 1) if step[0] == "q" else (kbd, ksum, 2)
                    pool.wait_ge(lm_done.sem, lm_done.at(i, n))
                    for k in range(KD):
                        spread(dst[:, k], src[:, k], head_mean[:]).then_inc(bd_done.sem, 1)
                elif step == ("lnB", 0):
                    layer_rstd(i, "b", 0)
                    read(pool, i, ("w1", 0), ("w1", 1))
                    read_before(pool, i, ("wx", 1))
                    add_row(x1b[:], x1[:], box_row).then_inc(x1b_done.sem, 1)
                elif step == ("lnB", 1):
                    layer_rstd(i, "b", 1)
                    read(pool, i, ("wx", 0), ("wx", 1))
                    read_before(pool, i, ("y3", 1))
                    add_row(base[:], x2[:], bfo3_row)
                    g.drain()
                    pool.wait_ge(xn_done["b"].sem, xn_done["b"].at(i, 2))
                    g.tensor_tensor(base[:], base[:], xn["b"], ALU.add).then_inc(base_done.sem, 1)

            run(pool, body)

        @block.scalar
        def _(act):
            s = nc.scalar
            for sig in act_makes:
                act.sem_inc(sig.sem, sig.per)
            act.wait_ge(consts_loaded, 16 * len(CONSTS))
            act.wait_ge(dve_consts, 1)

            def body(i, step):
                kind, n = step[0], step[1]
                x = stream(step)
                o = tile(step) if step in BANK else None
                if kind in ("xnTa", "xnTb"):
                    full(act, i, step)
                    done(s.activation(xnT[x][:, n % 2, :], o[:], ACT.Copy), step)
                elif kind == "q":
                    full(act, i, step)
                    done(s.activation(qT[:, n, :], o[:], ACT.Identity, bias=bq4_col[:, n:n + 1],
                                      scale=QK), step)
                elif kind == "k":
                    full(act, i, step)
                    done(s.activation(kT[:, n, :], o[:], ACT.Identity,
                                      bias=bqkv_col[:, 2 + n:3 + n]), step)
                elif kind == "s2":
                    read(act, i, step)
                    s.activation(attn2[:], attn2[:], ACT.Exp, scale=1.0 / LSEG).then_inc(e2_done.sem, 1)
                elif kind == "x2T":
                    full(act, i, step)
                    done(s.activation(attn2T[:], o[:].rearrange("p (a c) -> p a c", a=PAIRS), ACT.Copy),
                         step)
                elif kind == "s3":
                    act.wait_ge(nm3_done.sem, nm3_done.at(i, n + 1))
                    if n >= 2:
                        full(act, i, ("p3T", n - 2))
                    done(s.activation(p3[:, n % 2], o[:], ACT.Exp, bias=nm3[:, n:n + 1],
                                      accum_out=sum3[:, n:n + 1]), step)
                elif kind == "p3T":
                    full(act, i, step)
                    if n == 0:
                        full_before(act, i, ("o1", 1))
                    done(s.activation(p3T[:, n], o[:].rearrange("p (t c) -> p t c", t=T), ACT.Copy), step)
                elif kind == "zT":
                    full(act, i, step)
                    done(s.activation(zT[:, n, :], o[:, 0:P], ACT.Copy), step)
                elif kind == "a":
                    full(act, i, step)
                    q = slice(4 * n, 4 * n + 4)
                    s.activation(uz[:, q, 0:LM], o[:, 0:256].rearrange("p (a b) -> p a b", a=4), ACT.Copy)
                    done(s.activation(ut[:, q, :], o[:, 256:512].rearrange("p (a b) -> p a b", a=4),
                                      ACT.Copy), step)
                elif kind in ("s1", "sx"):
                    read(act, i, step)
                    t = p1[x][:, n % SLOTS]
                    s.activation(t, t, ACT.Exp).then_inc(p1_done[x].sem, 1)
                elif kind in ("p1T", "pxT"):
                    full(act, i, step)
                    if n == 0:
                        if x == "a":
                            full(act, i, ("z", 0))
                        else:
                            full_before(act, i, ("ox", 1))
                    done(s.activation(p1T[x][:, 4 * (n % 2):4 * (n % 2) + 4, (n // 2) * P:(n // 2 + 1) * P],
                                      o[:].rearrange("p (a b) -> p a b", a=4), ACT.Copy), step)
                elif kind == "qx":
                    full(act, i, step)
                    done(s.activation(qxT[:, n, :], o[:], ACT.Identity, bias=bqx_col[:, n:n + 1]), step)
                elif kind == "gate":
                    full(act, i, step)
                    done(s.activation(gate_h[:], o[:, 0:1], ACT.Gelu, bias=bp1_col[:]), step)
                elif kind == "logit":
                    act.wait_ge(sel_done.sem, sel_done.at(i, 1))
                    full_before(act, i, ("r", 1))
                    act.sem_inc(act_turn, 1)
                    read_before(act, i, ("r", 1))
                    act.sem_inc(act_turn, 1)
                    e = s.value_load(sel8[0:1, 0:1], min_val=0, max_val=7)
                    for dst, src in ((w1e[:], w1_dram[:, bass.ds(e * KD, KD), :]),
                                     (b1e[:], a["b1"][:, bass.ds(e * FM, FM)]),
                                     (w2e[:], w2_dram[:, bass.ds(e * FM, FM), :]),
                                     (b2e[:], a["b2"][:, bass.ds(e * KD, KD)])):
                        act.dma_start(dst, src).then_inc(expert_loaded.sem, 16)
                elif kind == "h":
                    if n == 0:
                        act.wait_ge(expert_loaded.sem, expert_loaded.at(i, 64))
                    full(act, i, step)
                    done(s.activation(hT[:, n, :], o[:], ACT.Gelu, bias=b1e[:, n:n + 1]), step)
                elif kind == "r":
                    full(act, i, step)
                    done(s.activation(rT[:, n, :], o[:], ACT.Identity, bias=b2e[:, n:n + 1]), step)

            run(act, body)

        @block.vector
        def _(dve):
            v = nc.vector
            for sig in dve_makes:
                dve.sem_inc(sig.sem, sig.per)
            dve.wait_ge(consts_loaded, 16 * len(CONSTS))
            dve.wait_ge(pool_consts, 1)
            v.tensor_scalar(bq4_col[:], bqkv_col[:, 0:2], QK, None, ALU.mult)
            v.tensor_scalar(bfo3_row[:], bfo_row[:], 0.3, None, ALU.mult)
            v.drain().then_inc(dve_consts, 1)

            def statistics(i, x, src):
                for t in range(T):
                    v.bn_stats(stats[x][:, t, :], src[:, t, :])
                v.drain()
                for t in range(T):
                    last = v.bn_aggr(mv[x][:, t, :], stats[x][:, t, :])
                last.then_inc(stats_done[x].sem, 1)

            def normalise(i, x, n, src):
                dve.wait_ge(rstd_done[x].sem, rstd_done[x].at(i, n + 1))
                for t in range(T):
                    last = v.tensor_scalar(xn[x][:, t, :], src[:, t, :], mv[x][:, t, 0:1],
                                           rstd[x][:, t:t + 1], ALU.subtract, ALU.mult)
                last.then_inc(xn_done[x].sem, 1)

            def quarter(step, w):
                return tile(step)[:, 0:4 * w].rearrange("p (a b) -> p a b", a=4)

            def body(i, step):
                kind, n = step[0], step[1]
                x = stream(step)
                o = tile(step) if step in BANK else None
                if kind == "kx":
                    dve.wait_ge(ctx_loaded.sem, ctx_loaded.at(i, 32))
                    full_before(dve, i, ("sx", 7))
                    v.tensor_scalar(key_mask[:], mask_in[:], 0, None, ALU.not_equal)
                    v.tensor_scalar(neg_row[:], mask_in[0:3, :], 0, neg_col[:], ALU.is_equal, ALU.mult)
                    v.drain().then_inc(key_mask_done.sem, 1)
                    full(dve, i, step)
                    dve.wait_ge(kxbd_done.sem, kxbd_done.before(i, 1))
                    for k in range(KD):
                        last = v.scalar_tensor_tensor(kxT[:, k, :], o[:, k * LM:(k + 1) * LM],
                                                      bkx_col[:, k:k + 1], key_mask[:], ALU.add, ALU.mult)
                    done(last, step)
                elif kind == "vx":
                    full(dve, i, step)
                    full_before(dve, i, ("ox", 1))
                    src = o[:, 0:D].rearrange("p (a h d) -> p a h d", a=PAIRS, h=2)
                    row = bvx_row[:].rearrange("p (a h d) -> p a h d", a=PAIRS, h=2)
                    for h in range(2):
                        q = slice(64 * h, 64 * h + 64)
                        last = v.tensor_tensor(vx_bd[q, :, DH * h:DH * h + DH], src[q, :, h], row[q, :, h],
                                               ALU.add)
                    done(last, step)
                elif kind == "lnA":
                    dve.wait_ge(x_loaded.sem, x_loaded.at(i, 16))
                    statistics(i, x, x_in)
                elif kind == "xnTa" and n == 0:
                    normalise(i, x, 0, x_in)
                elif step == ("lnB", 0):
                    read(dve, i, ("w1", 0), ("w1", 1))
                    statistics(i, x, x1)
                elif step == ("xnTb", 0):
                    dve.wait_ge(base_done.sem, base_done.before(i, 1))
                    normalise(i, x, 0, x1)
                elif step == ("lnB", 1):
                    read(dve, i, ("wx", 0), ("wx", 1))
                    statistics(i, x, x2)
                elif step == ("xnTb", 2):
                    normalise(i, x, 1, x2)
                elif kind in ("q", "k") and n == 1:
                    src, dst = (qT, qsum) if kind == "q" else (kT, ksum)
                    for k in range(KD):
                        read(dve, i, (kind, k))
                        last = v.tensor_reduce(dst[:, k, :], src[:, k, :].rearrange(
                            "p (m l) -> p m l", l=LSEG), AX.X, ALU.add)
                    last.then_inc(lm_done.sem, 1)
                elif kind == "v":
                    full(dve, i, step)
                    done(v.tensor_tensor(vt[:, 2 * n:2 * n + 2, :], o[:].rearrange("p (t d) -> p t d", t=2),
                                         bv_row[:].unsqueeze(1).broadcast_to([P, 2, D]), ALU.add), step)
                elif kind == "s2":
                    full(dve, i, step)
                    src = o[:].rearrange("p (a c) -> p a c", a=PAIRS)
                    v.tensor_reduce(m2[:], src, AX.X, ALU.max)
                    v.drain()
                    done(v.tensor_tensor(attn2[:], src, m2[:].unsqueeze(2).broadcast_to([P, PAIRS, LM]),
                                         ALU.subtract), step)
                elif kind == "x2T":
                    dve.wait_ge(e2_done.sem, e2_done.at(i, 1))
                    v.tensor_reduce(r2[:], attn2[:], AX.X, ALU.add)
                    v.drain()
                    v.reciprocal(r2[:], r2[:])
                    v.drain()
                    v.tensor_tensor(attn2[:], attn2[:], r2[:].unsqueeze(2).broadcast_to([P, PAIRS, LM]),
                                    ALU.mult).then_inc(attn2_done.sem, 1)
                elif kind == "s3":
                    full(dve, i, step)
                    v.tensor_reduce(nm3[:, n:n + 1], o[:], AX.X, ALU.max, negate=True)\
                        .then_inc(nm3_done.sem, 1)
                elif kind == "z":
                    read(dve, i, *[("s3", m) for m in range(PAIRS)])
                    v.reciprocal(r3[:], sum3[:])
                    v.drain()
                    full(dve, i, step)
                    src = o[:, 0:2 * P].rearrange("p (a h d) -> p a h d", a=PAIRS, h=2)
                    for h in range(2):
                        q = slice(64 * h, 64 * h + 64)
                        last = v.tensor_tensor(uz[q, :, LM:LM + DH], src[q, :, h],
                                               r3[q].unsqueeze(2).broadcast_to([64, PAIRS, DH]), ALU.mult)
                    done(last, step)
                elif kind in ("ps", "pe", "put", "puz"):
                    it, h = step[1:]
                    c = 3.25 ** -it
                    q = slice(4 * h, 4 * h + 4)
                    full(dve, i, step)
                    if kind == "ps":
                        ins = v.scalar_tensor_tensor(dd[:, q, :], uz[:, q, 0:LM], -7.0 * c,
                                                     quarter(step, LM), ALU.mult, ALU.add)
                    elif kind == "pe":
                        ins = v.scalar_tensor_tensor(gt[:, q, :], ut[:, q, :], 15.0 * c * c,
                                                     quarter(step, LM), ALU.mult, ALU.add)
                    elif kind == "put":
                        ins = v.scalar_tensor_tensor(ut[:, q, :], quarter(step, LM), -1.0 / (13.0 * c ** 3),
                                                     ut[:, q, :], ALU.mult, ALU.add)
                    else:
                        lo = 0 if it < ITERS - 1 else LM
                        ins = v.scalar_tensor_tensor(uz[:, q, lo:], quarter(step, LM + DH)[:, :, lo:],
                                                     -1.0 / (13.0 * c ** 3), uz[:, q, lo:],
                                                     ALU.mult, ALU.add)
                    done(ins, step)
                elif kind == "y":
                    full(dve, i, step)
                    src = o[:, 0:P].rearrange("p (a d) -> p a d", a=PAIRS)
                    for h in range(2):
                        q = slice(64 * h, 64 * h + 64)
                        last = v.tensor_scalar(y_bd[q, :, DH * h:DH * h + DH], src[q], 3.25 ** ITERS,
                                               None, ALU.mult)
                    done(last, step)
                elif kind in ("s1", "sx"):
                    full(dve, i, step)
                    src = o[:].rearrange("p (h c) -> p h c", h=8)
                    turned = "p1T" if x == "a" else "pxT"
                    if n >= SLOTS:
                        full(dve, i, (turned, n - SLOTS))
                    elif n == 0:
                        full_before(dve, i, (turned, 7))
                    m = m1[x][:, n % SLOTS]
                    v.tensor_reduce(m, src, AX.X, ALU.max)
                    v.drain()
                    done(v.tensor_tensor(p1[x][:, n % SLOTS], src, m.unsqueeze(2).broadcast_to([P, 8, LM]),
                                         ALU.subtract), step)
                elif kind in ("den1", "denx"):
                    full(dve, i, step)
                    done(v.reciprocal(rden[x][:, n], o[:]), step)
                elif kind in ("o1", "ox"):
                    full(dve, i, step)
                    read(dve, i, ("den1" if x == "a" else "denx", n))
                    done(v.tensor_tensor(oT[x][:, n, :], o[:], rden[x][:, n], ALU.mult), step)
                elif kind in ("w1", "wx"):
                    dst, res, sig = (x1, xr, xr_done) if kind == "w1" else (x2, x1b, x1b_done)
                    if n == 0:
                        dve.wait_ge(sig.sem, sig.at(i, 1))
                        nxt = x1b_done if kind == "w1" else base_done
                        dve.wait_ge(nxt.sem, nxt.before(i, 1))
                    full(dve, i, step)
                    q = slice(2 * n, 2 * n + 2)
                    done(v.tensor_tensor(dst[:, q, :], o[:].rearrange("p (t d) -> p t d", t=2),
                                         res[:, q, :], ALU.add), step)
                elif kind == "logit":
                    full(dve, i, step)
                    done(v.tensor_tensor(logits[:], o[0:1, 0:8], bp2_row[:], ALU.add), step)
                    v.drain()
                    v.max(top8[:], logits[:])
                    v.drain()
                    v.max_index(sel8[:], top8[:], logits[:]).then_inc(sel_done.sem, 1)
                elif kind == "y3":
                    if n == 0:
                        dve.wait_ge(base_done.sem, base_done.at(i, 1))
                        dve.wait_ge(stored.sem, stored.before(i, 16))
                    full(dve, i, step)
                    q = slice(2 * n, 2 * n + 2)
                    done(v.scalar_tensor_tensor(yo[:, q, :], o[:].rearrange("p (t d) -> p t d", t=2),
                                                0.3, base[:, q, :], ALU.mult, ALU.add), step)

            run(dve, body)

        @block.tensor
        def _(pe):
            mm = nc.tensor.matmul
            for sig in filled.values():
                pe.sem_inc(sig.sem, sig.per)
            pe.wait_ge(consts_loaded, 16 * len(CONSTS))
            pe.wait_ge(pool_consts, 1)

            def chain(dst, pairs):
                for k, (lhsT, rhs) in enumerate(pairs):
                    last = mm(dst, lhsT, rhs, start=(k == 0), stop=(k == len(pairs) - 1))
                return last

            def per_head(dst, lhsT, rhs, w, h):
                for j in range(4):
                    for r in range(2):
                        q = slice(64 * r, 64 * r + 64)
                        last = mm(dst[q, w * j:w * j + w], lhsT[q, 4 * h + j, 0:LM], rhs[q, 4 * h + j, 0:w],
                                  start=True, stop=True)
                return last

            def tokens(n):
                return n // 2, n % 2, slice((n // 2) * P, (n // 2 + 1) * P)

            def body(i, step):
                if step not in BANK:
                    return
                kind, n = step[0], step[1]
                o = tile(step)
                x = stream(step)

                def ready(*steps):
                    need = {BANK[step]: TURN[step]}
                    for m in steps:
                        need[BANK[m]] = max(need.get(BANK[m], 0), TURN[m] + 1)
                    for b, count in need.items():
                        pe.wait_ge(taken[b].sem, taken[b].at(i, count))

                if kind == "kx":
                    ready()
                    pe.wait_ge(ctx_loaded.sem, ctx_loaded.at(i, 32))
                    for m in range(KD):
                        last = chain(o[:, m * LM:(m + 1) * LM],
                                     [(wk[:, k, m * P:(m + 1) * P], ctxT[:, k, :]) for k in range(KD)])
                elif kind == "vx":
                    ready()
                    for r in range(2):
                        last = chain(o[64 * r:64 * r + 64, 0:D],
                                     [(ctxT[:, k, :], wv[:, k, :]) for k in range(KD)])
                elif kind in ("xnTa", "xnTb"):
                    ready()
                    pe.wait_ge(xn_done[x].sem, xn_done[x].at(i, n // 2 + 1))
                    for t in range(T):
                        last = nc.tensor.transpose(o[:, t * P:(t + 1) * P],
                                                   xn[x][:, t, (n % 2) * P:(n % 2 + 1) * P], ident[:])
                elif kind in ("q", "k"):
                    ready(("xnTa", 0), ("xnTa", 1))
                    c = (n + 2 * (kind == "k")) * P
                    last = chain(o[:], [(wqkv[:, k, c:c + P], xnT[x][:, k, :]) for k in range(KD)])
                elif kind == "v":
                    ready()
                    for t in range(2):
                        q = slice((2 * n + t) * P, (2 * n + t + 1) * P)
                        last = chain(o[:, t * D:(t + 1) * D],
                                     [(xnT[x][:, k, q], wqkv[:, k, 2 * D:3 * D]) for k in range(KD)])
                elif kind == "s2":
                    ready()
                    pe.wait_ge(bd_done.sem, bd_done.at(i, 2))
                    pe.wait_ge(lm_done.sem, lm_done.at(i, 2))
                    for j in range(PAIRS):
                        last = mm(o[:, j * LM:(j + 1) * LM], pair_of(qbd, j), ksum[:, j // 4, :],
                                  start=True, stop=True)
                elif kind == "s3":
                    ready()
                    if n == 0:
                        pe.wait_ge(bd_done.sem, bd_done.at(i, 1))
                    last = mm(o[:], pair_of(qbd, n), kT[:, n // 4, :], start=True, stop=True)
                elif kind == "x2T":
                    ready()
                    pe.wait_ge(attn2_done.sem, attn2_done.at(i, 1))
                    pe.sem_inc(pe_turn, 1)
                    for j in range(PAIRS):
                        for r in range(2):
                            q = slice(64 * r, 64 * r + 64)
                            last = mm(o[q, j * LM:(j + 1) * LM], attn2[q, j, :], ident[q, q],
                                      start=True, stop=True)
                elif kind == "p3T":
                    ready(("s3", n))
                    for t in range(T):
                        last = nc.tensor.transpose(o[:, t * P:(t + 1) * P],
                                                   p3[:, n % 2, t * P:(t + 1) * P], ident[:])
                elif kind == "a":
                    ready(("x2T", 0))
                    pe.sem_inc(pe_turn, 1)
                    per_head(o, attn2T, attn2, LM, n)
                    last = per_head(o[:, 256:512], attn2, attn2T, LM, n)
                elif kind == "zT":
                    ready(*[("p3T", 4 * n + j) for j in range(4)], ("v", 0), ("v", 1))
                    for t in range(T):
                        for j in range(4):
                            c = (4 * n + j) * 2 * DH
                            last = mm(o[32 * j:32 * j + 32, 0:P], vt[:, t, c:c + 2 * DH], p3T[:, 4 * n + j, t, :],
                                      start=(t == 0), stop=(t == T - 1))
                elif kind == "z":
                    ready(("zT", 0), ("zT", 1))
                    for j in range(2):
                        last = nc.tensor.transpose(o[:, j * P:(j + 1) * P], zT[:, j, :], ident[:])
                elif kind == "ps":
                    it, h = step[1:]
                    if it == 0:
                        ready(("a", h), ("z", 0))
                    else:
                        ready(("put", it - 1, h), ("puz", it - 1, h))
                    pe.sem_inc(pe_turn, 1)
                    last = per_head(o, ut, uz, LM, h)
                elif kind == "pe":
                    it, h = step[1:]
                    ready(("ps", it, h))
                    pe.sem_inc(pe_turn, 1)
                    last = per_head(o, dd, ut, LM, h)
                elif kind == "put":
                    it, h = step[1:]
                    ready(("pe", it, h))
                    pe.sem_inc(pe_turn, 1)
                    last = per_head(o, uz, gt, LM, h)
                elif kind == "puz":
                    it, h = step[1:]
                    ready(("pe", it, h))
                    pe.sem_inc(pe_turn, 1)
                    w = LM + DH
                    if it < ITERS - 1:
                        last = per_head(o, gt, uz, w, h)
                    else:
                        for j in range(4):
                            for r in range(2):
                                q = slice(64 * r, 64 * r + 64)
                                last = mm(o[q, w * j + LM:w * j + w], gt[q, 4 * h + j, :],
                                          uz[q, 4 * h + j, LM:w], start=True, stop=True)
                elif kind == "y":
                    ready(("puz", ITERS - 1, 0), ("puz", ITERS - 1, 1))
                    pe.sem_inc(pe_turn, 1)
                    for j in range(PAIRS):
                        for r in range(2):
                            q = slice(64 * r, 64 * r + 64)
                            last = mm(o[q, j * DH:(j + 1) * DH], attn2T[q, j, :], uz[q, j, LM:LM + DH],
                                      start=True, stop=True)
                elif kind == "s1":
                    ready()
                    if n == 0:
                        pe.wait_ge(bd_done.sem, bd_done.at(i, 4))
                    t, k, q = tokens(n)
                    last = mm(o[:], qT[:, k, q], kbd[:, k].rearrange("p h c -> p (h c)"),
                              start=True, stop=True)
                elif kind in ("p1T", "pxT"):
                    ready()
                    pe.wait_ge(p1_done[x].sem, p1_done[x].at(i, n + 1))
                    pT = p1[x][:, n % SLOTS].rearrange("p h c -> p (h c)")
                    for j in range(4):
                        last = nc.tensor.transpose(o[:, j * P:(j + 1) * P], pT[:, j * P:(j + 1) * P], ident[:])
                elif kind in ("den1", "denx", "o1", "ox"):
                    if kind[0] == "d":
                        turned = "p1T" if x == "a" else "pxT"
                        ready(*[(turned, m) for m in range(8)])
                    else:
                        ready(("y", 0) if x == "a" else ("vx", 0))
                    for j in range(4):
                        w = ones_bd[:] if kind[0] == "d" else (y_bd if x == "a" else vx_bd)[:, 4 * n + j, :]
                        last = mm(o[32 * j:32 * j + 32, :], w, p1T[x][:, 4 * n + j, :], start=True, stop=True)
                elif kind in ("w1", "wx"):
                    ready(*[("o1" if x == "a" else "ox", m) for m in range(2)])
                    for t in range(2):
                        q = slice((2 * n + t) * P, (2 * n + t + 1) * P)
                        w = wout if kind == "w1" else wo
                        last = chain(o[:, t * D:(t + 1) * D],
                                     [(oT[x][:, k, q], w[:, k, :]) for k in range(KD)])
                elif kind == "qx":
                    ready(("xnTb", 0), ("xnTb", 1))
                    last = chain(o[:], [(wq[:, k, n * P:(n + 1) * P], xnT[x][:, k, :]) for k in range(KD)])
                elif kind == "sx":
                    t, k, q = tokens(n)
                    ready(("qx", 0), ("qx", 1))
                    if n == 0:
                        pe.wait_ge(kxbd_done.sem, kxbd_done.at(i, 1))
                    mm(o[:], qxT[:, k, q], kx_bd[:, k].rearrange("p h c -> p (h c)"),
                       start=True, stop=False)
                    last = mm(o[:], ones3[:], neg_row[:].unsqueeze(1).broadcast_to([3, 8, LM]),
                              start=False, stop=True)
                elif kind == "gate":
                    ready(("xnTb", 2), ("xnTb", 3))
                    last = chain(o[:, 0:1], [(wp1[:, k, :], xnT[x][:, k, S - 1:S]) for k in range(KD)])
                elif kind == "logit":
                    ready(("gate", 0))
                    last = mm(o[0:1, 0:8], gate_h[:], wp2[:], start=True, stop=True)
                elif kind == "h":
                    ready()
                    if n == 0:
                        pe.wait_ge(expert_loaded.sem, expert_loaded.at(i, 64))
                    last = chain(o[:], [(w1e[:, k, n * P:(n + 1) * P], xnT[x][:, k, :]) for k in range(KD)])
                elif kind == "r":
                    ready(*[("h", m) for m in range(FM)])
                    last = chain(o[:], [(w2e[:, k, n * P:(n + 1) * P], hT[:, k, :]) for k in range(FM)])
                elif kind == "y3":
                    ready(("r", 0), ("r", 1))
                    for t in range(2):
                        q = slice((2 * n + t) * P, (2 * n + t + 1) * P)
                        last = chain(o[:, t * D:(t + 1) * D],
                                     [(rT[:, k, q], wfo[:, k, :]) for k in range(KD)])
                last.then_inc(filled[x].sem, 1)

            def pair_of(t, x):
                return t[:, x // 4, 2 * (x % 4):2 * (x % 4) + 2, :].rearrange("p h c -> p (h c)")

            run(pe, body)


def kernel(**inputs):
    import numpy as _np
    import concourse.bacc as _bacc
    from concourse import mybir as _mybir
    from concourse.bass_utils import run_bass_kernel_spmd as _run

    def get(name):
        return _np.asarray(inputs[name])

    def cols(v):
        v = v.reshape(-1, 128)
        return v.T

    def rows(v):
        return _np.broadcast_to(v[None, :], (128, v.shape[0]))

    layout = {
        "x": get("x"),
        "ctxT": get("ctx_1024").transpose(0, 2, 1),
        "mask": rows(get("mask_Bx1x1xS2_ik0").reshape(-1)),
        "Wqkv": get("L0_attn_Wqkv"),
        "bqkv": cols(get("L0_attn_bqkv")),
        "bv": rows(get("L0_attn_bqkv")[512:768]),
        "Wout": get("L0_attn_Wout"),
        "bout": rows(get("L0_attn_bout")),
        "WqT": get("L0_xattn_Wq").T,
        "bqx": cols(get("L0_xattn_bq")),
        "WkT": get("L0_xattn_Wk").T,
        "bkx": cols(get("L0_xattn_bk")),
        "WvT": get("L0_xattn_Wv").T,
        "bvx": rows(get("L0_xattn_bv")),
        "WoT": get("L0_xattn_Wo").T,
        "box": rows(get("L0_xattn_bo")),
        "Wp1": get("L0_ffn_Wp1"),
        "bp1": cols(get("L0_ffn_bp1")),
        "Wp2": get("L0_ffn_Wp2"),
        "bp2": get("L0_ffn_bp2")[None, :],
        "W1": get("L0_ffn_W1"),
        "b1": cols(get("L0_ffn_b1")),
        "W2": get("L0_ffn_W2"),
        "b2": cols(get("L0_ffn_b2")),
        "Wfo": get("L0_ffn_Wo"),
        "bfo": rows(get("L0_ffn_bo")),
    }
    nc = _bacc.Bacc("TRN2", target_bir_lowering=False, num_devices=1)
    arrays, aps = {}, {}
    for name, arr in layout.items():
        arr = _np.ascontiguousarray(arr)
        arrays[f"in_{name}"] = arr
        aps[name] = nc.dram_tensor(f"in_{name}", arr.shape, _mybir.dt.from_np(arr.dtype),
                                   kind="ExternalInput").ap()
    out = nc.dram_tensor("out_0", get("x").shape, _mybir.dt.float32, kind="ExternalOutput").ap()
    decoder_kernel(nc, aps, out)
    r = _run(nc, [arrays], core_ids=[0])
    return r.results[0]["out_0"]
```

```python
from contextlib import ExitStack

import concourse.bass as bass
from concourse import mybir

ALU = mybir.AluOpType
ACT = mybir.ActivationFunctionType
AX = mybir.AxisListType
F32 = mybir.dt.float32
BF16 = mybir.dt.bfloat16
I32 = mybir.dt.int32
U32 = mybir.dt.uint32

P = 128
HEADS = 16
DH = 16
LM = 64
PAIRS = HEADS // 2
ITERS = 6
BANKS = 8
SLOTS = 3
EPS = 1e-5
NEG_PARTS = (-998244352.0, -1753088.0, -2560.0)
assert sum(NEG_PARTS) == -1e9


def softmax_steps(scores, turned, lag=2):
    s = []
    for n in range(8 + lag):
        if n < 8:
            s.append((scores, n))
        if n >= lag:
            s.append((turned, n - lag))
    return s


NO_TILE = ("lnA", "soft2", "rec1", "lnB", "nmB", "recx")


def attention_steps():
    s = [("lnA", 0), ("xnTa", 0), ("xnTa", 1)]
    s += [("q", 0), ("q", 1), ("k", 0), ("k", 1), ("v", 0), ("v", 1)]
    s += [("s3", 0), ("s3", 1), ("s2", 0), ("p3T", 0), ("s3", 2), ("p3T", 1)]
    s += [("s3", 3), ("p3T", 2), ("soft2", 0), ("s3", 4), ("p3T", 3), ("s3", 5), ("zT", 0), ("p3T", 4)]
    s += [("s3", 6), ("p3T", 5), ("s3", 7), ("p3T", 6), ("x2T", 0), ("p3T", 7)]
    pairs = softmax_steps("s1", "p1T")
    return s + pairs[:1] + [("zT", 1)] + pairs[1:3] + [("z", 0)] + pairs[3:] + [("den1", 0), ("den1", 1)] + [
        ("rec1", 0, 0), ("rec1", 0, 1), ("rec1", 1, 0), ("rec1", 1, 1)]


def inverse_steps():
    s = [("a", 0), ("a", 1)]
    for it in range(ITERS):
        s += [("ps", it, 0), ("ps", it, 1), ("pe", it, 0), ("pe", it, 1)]
        for h in range(2):
            if it < ITERS - 1:
                s.append(("put", it, h))
            s.append(("puz", it, h))
    return s + [("y", 0), ("o1", 0), ("o1", 1), ("w1", 0), ("w1", 1)]


def rest_steps():
    s = [("kx", 0), ("vx", 0), ("xnTb", 0), ("xnTb", 1), ("qx", 0), ("qx", 1)]
    s += softmax_steps("sx", "pxT")
    s += [("denx", 0), ("denx", 1), ("recx", 0, 0), ("recx", 0, 1), ("recx", 1, 0), ("recx", 1, 1)]
    s += [("ox", 0), ("ox", 1), ("wx", 0), ("wx", 1)]
    s += [("lnB", 1), ("nmB", 1), ("xnTb", 2), ("xnTb", 3), ("gate", 0), ("logit", 0)]
    return s


def expert_steps():
    return [("h", m) for m in range(4)] + [("r", 0), ("r", 1), ("y3", 0), ("y3", 1)]


STEP_WEIGHT = {
    "lnA": 0, "soft2": 0, "nmB": 0, "rec1": 1, "recx": 1.18, "xnTa": 0.7, "q": 3.32, "k": 0.66,
    "v": 2.02, "s2": 3.32, "s3": 0.9, "x2T": 0.87, "p3T": 0.5, "a": 1.2, "zT": 0.64, "z": 0.12,
    "ps": 0.5, "pe": 0.21, "put": 0.75, "puz": 0.5, "y": 1.68, "s1": 0.9, "p1T": 0.7, "den1": 1.08,
    "o1": 0.9, "w1": 1.7, "kx": 0.65, "vx": 1.26, "lnB": 0, "xnTb": 0.59, "qx": 0.69, "sx": 1.1,
    "pxT": 0.59, "denx": 0.46, "ox": 1.49, "wx": 2.38, "gate": 0.48, "logit": 0.4, "h": 1.7,
    "r": 4.76, "y3": 1.71,
}
LEAD_WEIGHT = {
    ("lnA", 0): 2, ("xnTa", 0): 5.5, ("k", 0): 0.5, ("v", 0): 4, ("s3", 0): 1, ("s3", 1): 1.5,
    ("s3", 4): 1, ("p3T", 3): 1, ("s3", 7): 3, ("p3T", 6): 1, ("p3T", 7): 1, ("s1", 0): 0.5,
    ("z", 0): 1, ("p1T", 1): 1, ("s1", 4): 0.5, ("p1T", 7): 1, ("den1", 1): 0.5,
    ("put", 0, 0): 0.5, ("puz", 0, 0): 3, ("pe", 1, 0): 1, ("pe", 1, 1): 3.5, ("put", 2, 0): 1,
    ("ps", 3, 0): 2, ("pe", 3, 0): 0.5, ("pe", 3, 1): 3, ("puz", 3, 1): 0.5, ("ps", 4, 1): 0.5,
    ("pe", 4, 1): 4.5, ("puz", 4, 1): 3, ("pe", 5, 1): 0.5, ("y", 0): 1, ("o1", 1): 0.5,
    ("w1", 0): 0.5, ("lnB", 0): 1.5, ("y3", 1): 0.5, ("vx", 0): 2, ("xnTb", 1): 3.5, ("qx", 0): 2,
    ("sx", 0): 0.5, ("sx", 3): 0.5, ("pxT", 2): 2, ("sx", 5): 2, ("denx", 0): 2, ("denx", 1): 1,
    ("ox", 0): 4, ("wx", 0): 2.5, ("lnB", 1): 1, ("nmB", 1): 3, ("xnTb", 2): 3, ("gate", 0): 2,
    ("logit", 0): 1,
}


def interleave(*streams):
    timed = []
    for x, (steps, begin, end) in enumerate(streams):
        now, starts = 0.0, []
        for step in steps:
            now += LEAD_WEIGHT.get(step, 0)
            starts.append(starts[-1] if step[0] == "h" and step[1] else now)
            now += STEP_WEIGHT[step[0]]
        timed += [(begin + (end - begin) * t / now, x, n, step)
                  for n, (t, step) in enumerate(zip(starts, steps))]
    return [t[3] for t in sorted(timed)]


A_STEPS, C_STEPS, E_STEPS = attention_steps(), inverse_steps(), expert_steps()
B_STEPS = [("lnB", 0)] + rest_steps()
EB_STEPS = E_STEPS[:4] + [("lnB", 0)] + E_STEPS[4:] + rest_steps()
A_SPAN, C_SPAN, B_SPAN = (0.02, 1), (0.02, 0.69), (0.06, 0.95)
A_C_STEPS = interleave((A_STEPS, *A_SPAN), (C_STEPS, *C_SPAN))
A_C_B_STEPS = interleave((A_STEPS, *A_SPAN), (C_STEPS, *C_SPAN), (B_STEPS, *B_SPAN))
A_C_EB_STEPS = interleave((A_STEPS, *A_SPAN), (C_STEPS, *C_SPAN), (EB_STEPS, *B_SPAN))
C_EB_STEPS = interleave((C_STEPS, *C_SPAN), (EB_STEPS, *B_SPAN))
for _earlier, _later in ((("a", 1), ("s2", 0)), (("y", 0), ("x2T", 0)), (("y", 0), ("z", 0)),
                         (("w1", 1), ("s1", 0)), (("w1", 1), ("den1", 0)), (("lnB", 0), ("w1", 0))):
    for _steps in (A_C_STEPS, A_C_B_STEPS, A_C_EB_STEPS):
        if _earlier in _steps:
            assert _steps.index(_earlier) < _steps.index(_later), (_earlier, _later)
A_BANKS, C_BANKS, B_BANKS = (0, 1, 2), (3, 4), (5, 6, 7)
IN_B, IN_C, IN_E = {*EB_STEPS}, set(C_STEPS), set(E_STEPS)
FILL, BANK, TURN, USES = {}, {}, {}, [0] * BANKS
for _steps, _banks in ((A_STEPS, A_BANKS), (C_STEPS, C_BANKS), (B_STEPS + E_STEPS, B_BANKS)):
    for _n, _step in enumerate(x for x in _steps if x[0] not in NO_TILE):
        FILL[_step] = _n
        BANK[_step] = _banks[_n % len(_banks)]
        TURN[_step] = _n // len(_banks)
        USES[BANK[_step]] += 1


class Signal:

    def __init__(self, sem, per):
        self.sem, self.per = sem, per

    def at(self, i, k):
        return (i + 1) * self.per + k

    def before(self, i, k):
        return i * self.per + k


def decoder_kernel(nc, a, out):
    B, S, D = a["x"].shape
    T = S // P
    KD = D // P
    FF = 512
    FM = FF // P
    LSEG = S // LM
    QK = 0.25

    with ExitStack() as ctx:
        def sb(name, shape, dt=F32):
            return ctx.enter_context(nc.sbuf_tensor(name, shape, dt))

        def sem(name):
            return ctx.enter_context(nc.semaphore(name))

        bank = [ctx.enter_context(nc.psum_tensor(f"bank{b}", [P, 512], F32)) for b in range(BANKS)]

        wqkv = sb("wqkv", [P, KD, 3 * D])
        wout = sb("wout", [P, KD, D])
        wq = sb("wq", [P, KD, D])
        wk = sb("wk", [P, KD, D])
        wv = sb("wv", [P, KD, D])
        wo = sb("wo", [P, KD, D])
        wp1 = sb("wp1", [P, KD, P])
        wp2 = sb("wp2", [P, 8])
        wfo = sb("wfo", [P, KD, D])
        bqkv_col = sb("bqkv_col", [P, 6])
        bq4_col = sb("bq4_col", [P, 2])
        bqx_col = sb("bqx_col", [P, 2])
        bkx_col = sb("bkx_col", [P, 2])
        bp1_col = sb("bp1_col", [P, 1])
        bp2_row = sb("bp2_row", [1, 8])
        bv_row = sb("bv_row", [P, D])
        bout_row = sb("bout_row", [P, D])
        bvx_row = sb("bvx_row", [P, D])
        box_row = sb("box_row", [P, D])
        bfo_row = sb("bfo_row", [P, D])
        bfo3_row = sb("bfo3_row", [P, D])
        ident = sb("ident", [P, P])
        head_mask = sb("head_mask", [P, 8])
        head_mean = sb("head_mean", [P, 8])
        ones_bd = sb("ones_bd", [P, 32])
        ones3 = sb("ones3", [3, P], BF16)
        neg_col = sb("neg_col", [3, 1])
        x_in = sb("x_in", [P, T, D])
        xr = sb("xr", [P, T, D])
        stats = {x: sb(f"stats_{x}", [P, T, 6]) for x in "ab"}
        mv = {x: sb(f"mv_{x}", [P, T, 2]) for x in "ab"}
        var_eps = {x: sb(f"var_eps_{x}", [P, T]) for x in "ab"}
        rstd = {x: sb(f"rstd_{x}", [P, T]) for x in "ab"}
        xn = {x: sb(f"xn_{x}", [P, T, D]) for x in "ab"}
        xnT = {x: sb(f"xnT_{x}", [P, KD, S]) for x in "ab"}
        m1 = {x: sb(f"m1_{x}", [P, SLOTS, 8]) for x in "ab"}
        p1 = {x: sb(f"p1_{x}", [P, SLOTS, 8, LM]) for x in "ab"}
        p1T = {x: sb(f"p1T_{x}", [P, PAIRS, S]) for x in "ab"}
        oT = {x: sb(f"oT_{x}", [P, KD, S]) for x in "ab"}
        minus_half = sb("minus_half", [P, T])
        qT = sb("qT", [P, KD, S])
        kT = sb("kT", [P, KD, S])
        vt = sb("vt", [P, T, D])
        qsum = sb("qsum", [P, KD, LM])
        ksum = sb("ksum", [P, KD, LM])
        qbd = sb("qbd", [P, KD, 8, LM])
        kbd = sb("kbd", [P, KD, 8, LM])
        m2 = sb("m2", [P, PAIRS])
        r2 = sb("r2", [P, PAIRS])
        attn2 = sb("attn2", [P, PAIRS, LM])
        attn2T = sb("attn2T", [P, PAIRS, LM])
        nm3 = sb("nm3", [P, PAIRS])
        sum3 = sb("sum3", [P, PAIRS])
        r3 = sb("r3", [P, PAIRS])
        zT = sb("zT", [P, 2, P])
        p3 = sb("p3", [P, 2, S])
        p3T = sb("p3T", [P, 4, T, P])
        uz = sb("uz", [P, PAIRS, LM + DH])
        ut = sb("ut", [P, PAIRS, LM])
        dd = sb("dd", [P, PAIRS, LM])
        gt = sb("gt", [P, PAIRS, LM])
        y_bd = sb("y_bd", [P, PAIRS, 32])
        x1 = sb("x1", [P, T, D])
        x1b = sb("x1b", [P, T, D])
        ctxT = sb("ctxT", [P, KD, LM])
        mask_in = sb("mask_in", [P, LM], I32)
        key_mask = sb("key_mask", [P, LM])
        neg_row = sb("neg_row", [3, LM], BF16)
        kxT = sb("kxT", [P, KD, LM])
        kx_bd = sb("kx_bd", [P, KD, 8, LM])
        vx_bd = sb("vx_bd", [P, PAIRS, 32])
        qxT = sb("qxT", [P, KD, S])
        x2 = sb("x2", [P, T, D])
        base = sb("base", [P, T, D])
        gate_h = sb("gate_h", [P, 1])
        logits = sb("logits", [1, 8])
        top8 = sb("top8", [1, 8])
        sel8 = sb("sel8", [1, 8], U32)
        w1e = sb("w1e", [P, KD, FF])
        w2e = sb("w2e", [P, FM, D])
        b1e = sb("b1e", [P, FM])
        b2e = sb("b2e", [P, KD])
        hT = sb("hT", [P, FM, S])
        rT = qxT

        filled = {"a": Signal(sem("a_tiles_filled"), sum(x not in IN_B | IN_C for x in FILL)),
                  "b": Signal(sem("b_tiles_filled"), sum(x in IN_B for x in FILL)),
                  "c": Signal(sem("c_tiles_filled"), sum(x in IN_C for x in FILL))}
        taken = [Signal(sem(f"bank{b}_taken"), USES[b]) for b in range(BANKS)]
        first_consts_loaded = sem("first_consts_loaded")
        consts_loaded = sem("consts_loaded")
        x_loaded = Signal(sem("x_loaded"), 16)
        ctx_loaded = Signal(sem("ctx_loaded"), 32)
        expert_loaded = Signal(sem("expert_loaded"), 64)
        stored = Signal(sem("stored"), 16)
        pool_consts = sem("pool_consts")
        dve_consts = sem("dve_consts")
        bfo3_done = sem("bfo3_done")
        stats_done = {"a": Signal(sem("a_stats_done"), 1), "b": Signal(sem("b_stats_done"), 2)}
        rstd_done = {"a": Signal(sem("a_rstd_done"), 1), "b": Signal(sem("b_rstd_done"), 2)}
        xn_done = {"a": Signal(sem("a_xn_done"), 1), "b": Signal(sem("b_xn_done"), 1)}
        xn3_done = Signal(sem("xn3_done"), 1)
        p1_done = {"a": Signal(sem("a_p1_done"), 8), "b": Signal(sem("b_p1_done"), 8)}
        lm_done = Signal(sem("lm_done"), 2)
        bd_done = Signal(sem("bd_done"), 4)
        e2_done = Signal(sem("e2_done"), 1)
        attn2_done = Signal(sem("attn2_done"), 1)
        nm3_done = Signal(sem("nm3_done"), PAIRS)
        xr_done = Signal(sem("xr_done"), 1)
        x1b_done = Signal(sem("x1b_done"), 1)
        base_done = Signal(sem("base_done"), 1)
        key_mask_done = Signal(sem("key_mask_done"), 1)
        kxbd_done = Signal(sem("kxbd_done"), 1)
        sel_done = Signal(sem("sel_done"), 1)
        pe_turn, act_turn = sem("pe_turn"), sem("act_turn")
        pool_turn, sp_turn = sem("pool_turn"), sem("sp_turn")

        dve_makes = [*stats_done.values(), xn3_done, lm_done, attn2_done, nm3_done,
                     key_mask_done, sel_done, *taken]
        act_makes = [*p1_done.values(), e2_done, expert_loaded]
        pool_makes = [*rstd_done.values(), *xn_done.values(), bd_done, xr_done, x1b_done, base_done, kxbd_done]

        def stream(step):
            return "b" if step in IN_B else "c" if step in IN_C else "a"

        def tile(step):
            return bank[BANK[step]]

        def done(ins, step):
            return ins.then_inc(taken[BANK[step]].sem, 1)

        def full(eng, i, step):
            f = filled[stream(step)]
            eng.wait_ge(f.sem, f.at(i, FILL[step] + 1))

        def full_before(eng, i, step):
            f = filled[stream(step)]
            eng.wait_ge(f.sem, f.before(i, FILL[step] + 1))

        def read(eng, i, *steps):
            for b in sorted({BANK[s] for s in steps}):
                turn = max(TURN[s] for s in steps if BANK[s] == b)
                eng.wait_ge(taken[b].sem, taken[b].at(i, turn + 1))

        def read_before(eng, i, step):
            f = taken[BANK[step]]
            eng.wait_ge(f.sem, f.before(i, TURN[step] + 1))

        def run(eng, body, rest=lambda: None):
            def turn(steps, i):
                for step in steps:
                    back = 3 if step in IN_E else 2 if step in IN_B else 1 if step in IN_C else 0
                    body(i - back, step)

            turn(A_STEPS, 0)
            eng.wait_ge(consts_loaded, 16 * len(CONSTS))
            rest()
            turn(A_C_STEPS, 1)
            turn(A_C_B_STEPS, 2)
            with eng.Fori(3, B) as i:
                turn(A_C_EB_STEPS, i)
            turn(C_EB_STEPS, B)
            turn(EB_STEPS, B + 1)
            turn(E_STEPS, B + 2)

        block = ctx.enter_context(nc.Block())
        x_dram = a["x"].rearrange("b (t p) d -> p (b t) d", p=P)
        out_dram = out.rearrange("b (t p) d -> p (b t) d", p=P)
        ctx_dram = a["ctxT"].rearrange("b (k p) c -> p (b k) c", p=P)
        mask_dram = a["mask"]
        w1_dram = a["W1"].rearrange("e (k p) f -> p (e k) f", p=P)
        w2_dram = a["W2"].rearrange("e (k p) f -> p (e k) f", p=P)

        def halves(w):
            return w.rearrange("(k p) n -> p k n", p=P)

        FIRST_CONSTS = [(wqkv[:], halves(a["Wqkv"])), (bqkv_col[:], a["bqkv"]), (bv_row[:], a["bv"]),
                        (bout_row[:], a["bout"])]
        CONSTS = [
            (wk[:], halves(a["WkT"])), (wv[:], halves(a["WvT"])), (bkx_col[:], a["bkx"]),
            (bvx_row[:], a["bvx"]), (wout[:], halves(a["Wout"])),
            (wq[:], halves(a["WqT"])), (bqx_col[:], a["bqx"]), (wo[:], halves(a["WoT"])),
            (box_row[:], a["box"]), (wp1[:], halves(a["Wp1"])), (bp1_col[:], a["bp1"]),
            (wp2[:], a["Wp2"]), (bp2_row[:], a["bp2"]), (wfo[:], halves(a["Wfo"])),
            (bfo_row[:], a["bfo"]),
        ]

        @block.sync
        def _(sp):
            def load_x(i, first=False):
                if not first:
                    sp.wait_ge(xn_done["a"].sem, xn_done["a"].before(i, 1))
                    sp.sem_inc(sp_turn, 1)
                    sp.wait_ge(xr_done.sem, xr_done.before(i, 1))
                    sp.sem_inc(sp_turn, 1)
                sp.dma_start(x_in[:], x_dram[:, bass.ds(i * T, T), :]).then_inc(x_loaded.sem, 16)

            def load_context(i, first=False):
                if not first:
                    full_before(sp, i, ("vx", 0))
                    sp.sem_inc(sp_turn, 1)
                    sp.wait_ge(key_mask_done.sem, key_mask_done.before(i, 1))
                    sp.sem_inc(sp_turn, 1)
                sp.dma_start(ctxT[:], ctx_dram[:, bass.ds(i * KD, KD), :]).then_inc(ctx_loaded.sem, 16)
                sp.dma_start(mask_in[:], mask_dram[:, bass.ds(i * LM, LM)]).then_inc(ctx_loaded.sem, 16)

            def store(i):
                read(sp, i, ("y3", 0))
                sp.sem_inc(sp_turn, 1)
                read(sp, i, ("y3", 1))
                sp.sem_inc(sp_turn, 1)
                sp.dma_start(out_dram[:, bass.ds(i * T, T), :], base[:]).then_inc(stored.sem, 16)

            sp.sem_inc(x_loaded.sem, 16)
            sp.sem_inc(ctx_loaded.sem, 32)
            sp.sem_inc(stored.sem, 16)
            load_x(0, first=True)
            for dst, src in FIRST_CONSTS:
                sp.dma_start(dst, src).then_inc(first_consts_loaded, 16)
            for dst, src in CONSTS:
                sp.dma_start(dst, src).then_inc(consts_loaded, 16)
            load_context(0, first=True)
            load_x(1)
            load_x(2)
            load_context(1)
            load_x(3)
            with sp.Fori(3, B - 1) as i:
                store(i - 3)
                load_context(i - 1)
                load_x(i + 1)
            store(B - 4)
            load_context(B - 2)
            store(B - 3)
            load_context(B - 1)
            store(B - 2)
            store(B - 1)
            sp.wait_ge(stored.sem, stored.at(B - 1, 16))

        @block.gpsimd
        def _(pool):
            g = nc.gpsimd
            for s in pool_makes:
                pool.sem_inc(s.sem, s.per)
            g.memset(ident[:], 0.0)
            g.memset(head_mask[:], 1.0)
            g.memset(ones_bd[:], 0.0)
            g.memset(neg_col[:], NEG_PARTS[0])
            g.memset(y_bd[:], 0.0)
            g.memset(vx_bd[:], 0.0)
            g.memset(ones3[:], 1.0)
            g.memset(minus_half[:], -0.5)
            g.drain()
            g.affine_select(out=ident[:], in_=ident[:], compare_op=ALU.not_equal, fill=1.0,
                            base=0, pattern=[[-1, P]], channel_multiplier=1)
            g.affine_select(out=head_mask[:], in_=head_mask[:], compare_op=ALU.is_ge, fill=0.0,
                            base=0, pattern=[[-DH, 8]], channel_multiplier=1)
            g.drain()
            g.memset(ones_bd[0:64, 0:16], 1.0)
            g.drain()
            g.memset(ones_bd[64:128, 16:32], 1.0)
            g.drain()
            g.affine_select(out=neg_col[:], in_=neg_col[:], compare_op=ALU.not_equal,
                            fill=NEG_PARTS[1], base=-1, pattern=[[0, 1]], channel_multiplier=1)
            g.drain()
            g.affine_select(out=head_mask[:], in_=head_mask[:], compare_op=ALU.is_ge, fill=0.0,
                            base=DH - 1, pattern=[[DH, 8]], channel_multiplier=-1)
            g.affine_select(out=neg_col[:], in_=neg_col[:], compare_op=ALU.not_equal,
                            fill=NEG_PARTS[2], base=-2, pattern=[[0, 1]], channel_multiplier=1)
            g.drain()
            g.tensor_scalar(head_mean[:], head_mask[:], 1.0 / LSEG, None, ALU.mult)
            g.tensor_scalar(head_mask[:], head_mask[:], QK, None, ALU.mult)
            g.drain().then_inc(pool_consts, 1)
            pool.wait_ge(first_consts_loaded, 16 * len(FIRST_CONSTS))
            pool.wait_ge(dve_consts, 1)

            def layer_rstd(i, x, n):
                pool.wait_ge(stats_done[x].sem, stats_done[x].at(i, n + 1))
                pool.sem_inc(pool_turn, 1)
                g.tensor_scalar(var_eps[x][:], mv[x][:, :, 1], EPS, None, ALU.add)
                g.drain()
                g.tensor_tensor(rstd[x][:], var_eps[x][:], minus_half[:], ALU.pow)\
                    .then_inc(rstd_done[x].sem, 1)

            def normalise(x, src):
                for t in range(T):
                    last = g.tensor_scalar(xn[x][:, t, :], src[:, t, :], mv[x][:, t, 0:1],
                                           rstd[x][:, t:t + 1], ALU.subtract, ALU.mult)
                last.then_inc(xn_done[x].sem, 1)

            def spread(dst, src, scale):
                return g.tensor_tensor(dst, src.unsqueeze(1).broadcast_to([P, 8, LM]),
                                       scale.unsqueeze(2).broadcast_to([P, 8, LM]), ALU.mult)

            def add_row(dst, src, row):
                return g.tensor_tensor(dst, src, row[:].unsqueeze(1).broadcast_to([P, T, D]), ALU.add)

            def body(i, step):
                if step == ("kx", 0):
                    read(pool, i, step)
                    full_before(pool, i, ("sx", 7))
                    for k in range(KD):
                        last = spread(kx_bd[:, k], kxT[:, k], head_mask[:])
                    last.then_inc(kxbd_done.sem, 1)
                elif step == ("lnA", 0):
                    layer_rstd(i, "a", 0)
                    g.drain()
                    normalise("a", x_in)
                elif step == ("s1", 0):
                    pool.wait_ge(x_loaded.sem, x_loaded.at(i, 16))
                    read_before(pool, i, ("w1", 1))
                    add_row(xr[:], x_in[:], bout_row).then_inc(xr_done.sem, 1)
                elif step == ("q", 1) or step == ("k", 1):
                    full_before(pool, i, ("s1", 7))
                    dst, src, n = (qbd, qsum, 1) if step[0] == "q" else (kbd, ksum, 2)
                    pool.wait_ge(lm_done.sem, lm_done.at(i, n))
                    for k in range(KD):
                        spread(dst[:, k], src[:, k], head_mean[:]).then_inc(bd_done.sem, 1)
                elif step == ("lnB", 0):
                    layer_rstd(i, "b", 0)
                    g.drain()
                    normalise("b", x1)
                    read(pool, i, ("w1", 0), ("w1", 1))
                    read_before(pool, i, ("wx", 1))
                    add_row(x1b[:], x1[:], box_row).then_inc(x1b_done.sem, 1)
                elif step == ("lnB", 1):
                    layer_rstd(i, "b", 1)
                    read(pool, i, ("wx", 0), ("wx", 1))
                    pool.wait_ge(stored.sem, stored.before(i, 16))
                    add_row(base[:], x2[:], bfo3_row)
                    g.drain()
                    pool.wait_ge(xn3_done.sem, xn3_done.at(i, 1))
                    g.tensor_tensor(base[:], base[:], xn["b"][:], ALU.add).then_inc(base_done.sem, 1)

            def rest():
                pool.wait_ge(bfo3_done, 1)

            run(pool, body, rest)

        @block.scalar
        def _(act):
            s = nc.scalar
            for sig in act_makes:
                act.sem_inc(sig.sem, sig.per)
            act.wait_ge(first_consts_loaded, 16 * len(FIRST_CONSTS))
            act.wait_ge(dve_consts, 1)

            def body(i, step):
                kind, n = step[0], step[1]
                x = "b" if step in IN_B else "a"
                o = tile(step) if step in BANK else None
                if kind in ("xnTa", "xnTb"):
                    full(act, i, step)
                    done(s.activation(xnT[x][:, n % 2, :], o[:], ACT.Copy), step)
                elif kind == "q":
                    full(act, i, step)
                    done(s.activation(qT[:, n, :], o[:], ACT.Identity, bias=bq4_col[:, n:n + 1],
                                      scale=QK), step)
                elif kind == "k":
                    full(act, i, step)
                    done(s.activation(kT[:, n, :], o[:], ACT.Identity,
                                      bias=bqkv_col[:, 2 + n:3 + n]), step)
                elif kind == "s2":
                    read(act, i, step)
                    s.activation(attn2[:], attn2[:], ACT.Exp, scale=1.0 / LSEG).then_inc(e2_done.sem, 1)
                elif kind == "x2T":
                    full(act, i, step)
                    full_before(act, i, ("y", 0))
                    done(s.activation(attn2T[:], o[:].rearrange("p (a c) -> p a c", a=PAIRS), ACT.Copy),
                         step)
                elif kind == "s3":
                    act.wait_ge(nm3_done.sem, nm3_done.at(i, n + 1))
                    if n >= 2:
                        full(act, i, ("p3T", n - 2))
                    done(s.activation(p3[:, n % 2], o[:], ACT.Exp, bias=nm3[:, n:n + 1],
                                      accum_out=sum3[:, n:n + 1]), step)
                elif kind == "p3T":
                    full(act, i, step)
                    if n == 4:
                        full(act, i, ("zT", 0))
                    done(s.activation(p3T[:, n % 4], o[:].rearrange("p (t c) -> p t c", t=T), ACT.Copy), step)
                elif kind == "zT":
                    full(act, i, step)
                    done(s.activation(zT[:, n, :], o[:, 0:P], ACT.Copy), step)
                elif kind == "a":
                    full(act, i, step)
                    q = slice(4 * n, 4 * n + 4)
                    s.activation(uz[:, q, 0:LM], o[:, 0:256].rearrange("p (a b) -> p a b", a=4), ACT.Copy)
                    done(s.activation(ut[:, q, :], o[:, 256:512].rearrange("p (a b) -> p a b", a=4),
                                      ACT.Copy), step)
                elif kind in ("s1", "sx"):
                    read(act, i, step)
                    t = p1[x][:, n % SLOTS]
                    s.activation(t, t, ACT.Exp).then_inc(p1_done[x].sem, 1)
                elif kind in ("p1T", "pxT"):
                    full(act, i, step)
                    if n == 0:
                        full_before(act, i, ("o1" if x == "a" else "ox", 1))
                    done(s.activation(p1T[x][:, 4 * (n % 2):4 * (n % 2) + 4, (n // 2) * P:(n // 2 + 1) * P],
                                      o[:].rearrange("p (a b) -> p a b", a=4), ACT.Copy), step)
                elif kind == "qx":
                    full(act, i, step)
                    done(s.activation(qxT[:, n, :], o[:], ACT.Identity, bias=bqx_col[:, n:n + 1]), step)
                elif kind == "gate":
                    full(act, i, step)
                    done(s.activation(gate_h[:], o[:, 0:1], ACT.Gelu, bias=bp1_col[:]), step)
                elif kind == "logit":
                    act.wait_ge(sel_done.sem, sel_done.at(i, 1))
                    full_before(act, i, ("r", 1))
                    act.sem_inc(act_turn, 1)
                    read_before(act, i, ("r", 1))
                    act.sem_inc(act_turn, 1)
                    e = s.value_load(sel8[0:1, 0:1], min_val=0, max_val=7)
                    for dst, src in ((w1e[:], w1_dram[:, bass.ds(e * KD, KD), :]),
                                     (b1e[:], a["b1"][:, bass.ds(e * FM, FM)]),
                                     (w2e[:], w2_dram[:, bass.ds(e * FM, FM), :]),
                                     (b2e[:], a["b2"][:, bass.ds(e * KD, KD)])):
                        act.dma_start(dst, src).then_inc(expert_loaded.sem, 16)
                elif kind == "h":
                    if n == 0:
                        act.wait_ge(expert_loaded.sem, expert_loaded.at(i, 64))
                    full(act, i, step)
                    done(s.activation(hT[:, n, :], o[:], ACT.Gelu, bias=b1e[:, n:n + 1]), step)
                elif kind == "r":
                    full(act, i, step)
                    done(s.activation(rT[:, n, :], o[:], ACT.Identity, bias=b2e[:, n:n + 1]), step)

            run(act, body)

        @block.vector
        def _(dve):
            v = nc.vector
            for sig in dve_makes:
                dve.sem_inc(sig.sem, sig.per)
            dve.wait_ge(first_consts_loaded, 16 * len(FIRST_CONSTS))
            dve.wait_ge(pool_consts, 1)
            v.tensor_scalar(bq4_col[:], bqkv_col[:, 0:2], QK, None, ALU.mult)
            v.drain().then_inc(dve_consts, 1)

            def statistics(i, x, src):
                for t in range(T):
                    v.bn_stats(stats[x][:, t, :], src[:, t, :])
                v.drain()
                for t in range(T):
                    last = v.bn_aggr(mv[x][:, t, :], stats[x][:, t, :])
                last.then_inc(stats_done[x].sem, 1)

            def normalise(i, x, src):
                dve.wait_ge(rstd_done[x].sem, rstd_done[x].at(i, 2))
                for t in range(T):
                    last = v.tensor_scalar(xn[x][:, t, :], src[:, t, :], mv[x][:, t, 0:1],
                                           rstd[x][:, t:t + 1], ALU.subtract, ALU.mult)
                last.then_inc(xn3_done.sem, 1)

            def quarter(step, w):
                return tile(step)[:, 0:4 * w].rearrange("p (a b) -> p a b", a=4)

            def body(i, step):
                kind, n = step[0], step[1]
                x = "b" if step in IN_B else "a"
                o = tile(step) if step in BANK else None
                if kind == "kx":
                    dve.wait_ge(ctx_loaded.sem, ctx_loaded.at(i, 32))
                    full_before(dve, i, ("sx", 7))
                    v.tensor_scalar(key_mask[:], mask_in[:], 0, None, ALU.not_equal)
                    v.tensor_scalar(neg_row[:], mask_in[0:3, :], 0, neg_col[:], ALU.is_equal, ALU.mult)
                    v.drain().then_inc(key_mask_done.sem, 1)
                    full(dve, i, step)
                    dve.wait_ge(kxbd_done.sem, kxbd_done.before(i, 1))
                    for k in range(KD):
                        last = v.scalar_tensor_tensor(kxT[:, k, :], o[:, k * LM:(k + 1) * LM],
                                                      bkx_col[:, k:k + 1], key_mask[:], ALU.add, ALU.mult)
                    done(last, step)
                elif kind == "vx":
                    full(dve, i, step)
                    full_before(dve, i, ("ox", 1))
                    src = o[:, 0:D].rearrange("p (a h d) -> p a h d", a=PAIRS, h=2)
                    row = bvx_row[:].rearrange("p (a h d) -> p a h d", a=PAIRS, h=2)
                    for h in range(2):
                        q = slice(64 * h, 64 * h + 64)
                        last = v.tensor_tensor(vx_bd[q, :, DH * h:DH * h + DH], src[q, :, h], row[q, :, h],
                                               ALU.add)
                    done(last, step)
                elif kind == "lnA":
                    dve.wait_ge(x_loaded.sem, x_loaded.at(i, 16))
                    statistics(i, x, x_in)
                elif step == ("lnB", 0):
                    read(dve, i, ("w1", 0), ("w1", 1))
                    statistics(i, x, x1)
                elif step == ("lnB", 1):
                    read(dve, i, ("wx", 0), ("wx", 1))
                    statistics(i, x, x2)
                elif step == ("nmB", 1):
                    normalise(i, x, x2)
                elif kind in ("q", "k") and n == 1:
                    src, dst = (qT, qsum) if kind == "q" else (kT, ksum)
                    for k in range(KD):
                        read(dve, i, (kind, k))
                        last = v.tensor_reduce(dst[:, k, :], src[:, k, :].rearrange(
                            "p (m l) -> p m l", l=LSEG), AX.X, ALU.add)
                    last.then_inc(lm_done.sem, 1)
                elif kind == "v":
                    full(dve, i, step)
                    done(v.tensor_tensor(vt[:, 2 * n:2 * n + 2, :], o[:].rearrange("p (t d) -> p t d", t=2),
                                         bv_row[:].unsqueeze(1).broadcast_to([P, 2, D]), ALU.add), step)
                elif kind == "s2":
                    full(dve, i, step)
                    full_before(dve, i, ("a", 1))
                    src = o[:].rearrange("p (a c) -> p a c", a=PAIRS)
                    v.tensor_reduce(m2[:], src, AX.X, ALU.max)
                    v.drain()
                    done(v.tensor_tensor(attn2[:], src, m2[:].unsqueeze(2).broadcast_to([P, PAIRS, LM]),
                                         ALU.subtract), step)
                elif kind == "soft2":
                    dve.wait_ge(e2_done.sem, e2_done.at(i, 1))
                    v.tensor_reduce(r2[:], attn2[:], AX.X, ALU.add)
                    v.drain()
                    v.reciprocal(r2[:], r2[:])
                    v.drain()
                    v.tensor_tensor(attn2[:], attn2[:], r2[:].unsqueeze(2).broadcast_to([P, PAIRS, LM]),
                                    ALU.mult).then_inc(attn2_done.sem, 1)
                elif kind == "s3":
                    full(dve, i, step)
                    v.tensor_reduce(nm3[:, n:n + 1], o[:], AX.X, ALU.max, negate=True)\
                        .then_inc(nm3_done.sem, 1)
                elif kind == "z":
                    read(dve, i, *[("s3", m) for m in range(PAIRS)])
                    v.reciprocal(r3[:], sum3[:])
                    v.drain()
                    full(dve, i, step)
                    full_before(dve, i, ("y", 0))
                    src = o[:, 0:2 * P].rearrange("p (a h d) -> p a h d", a=PAIRS, h=2)
                    for h in range(2):
                        q = slice(64 * h, 64 * h + 64)
                        last = v.tensor_tensor(uz[q, :, LM:LM + DH], src[q, :, h],
                                               r3[q].unsqueeze(2).broadcast_to([64, PAIRS, DH]), ALU.mult)
                    done(last, step)
                elif kind in ("ps", "pe", "put", "puz"):
                    it, h = step[1:]
                    c = 3.25 ** -it
                    q = slice(4 * h, 4 * h + 4)
                    full(dve, i, step)
                    if kind == "ps":
                        ins = v.scalar_tensor_tensor(dd[:, q, :], uz[:, q, 0:LM], -7.0 * c,
                                                     quarter(step, LM), ALU.mult, ALU.add)
                    elif kind == "pe":
                        ins = v.scalar_tensor_tensor(gt[:, q, :], ut[:, q, :], 15.0 * c * c,
                                                     quarter(step, LM), ALU.mult, ALU.add)
                    elif kind == "put":
                        ins = v.scalar_tensor_tensor(ut[:, q, :], quarter(step, LM), -1.0 / (13.0 * c ** 3),
                                                     ut[:, q, :], ALU.mult, ALU.add)
                    else:
                        lo = 0 if it < ITERS - 1 else LM
                        ins = v.scalar_tensor_tensor(uz[:, q, lo:], quarter(step, LM + DH)[:, :, lo:],
                                                     -1.0 / (13.0 * c ** 3), uz[:, q, lo:],
                                                     ALU.mult, ALU.add)
                    done(ins, step)
                elif kind == "y":
                    full(dve, i, step)
                    src = o[:, 0:P].rearrange("p (a d) -> p a d", a=PAIRS)
                    for h in range(2):
                        q = slice(64 * h, 64 * h + 64)
                        last = v.tensor_scalar(y_bd[q, :, DH * h:DH * h + DH], src[q], 3.25 ** ITERS,
                                               None, ALU.mult)
                    done(last, step)
                elif kind in ("s1", "sx"):
                    full(dve, i, step)
                    src = o[:].rearrange("p (h c) -> p h c", h=8)
                    turned = "p1T" if x == "a" else "pxT"
                    if n >= SLOTS:
                        full(dve, i, (turned, n - SLOTS))
                    elif n == 0:
                        full_before(dve, i, (turned, 7))
                    m = m1[x][:, n % SLOTS]
                    v.tensor_reduce(m, src, AX.X, ALU.max)
                    v.drain()
                    done(v.tensor_tensor(p1[x][:, n % SLOTS], src, m.unsqueeze(2).broadcast_to([P, 8, LM]),
                                         ALU.subtract), step)
                elif kind in ("rec1", "recx"):
                    den, part = ("den1" if x == "a" else "denx", n), step[2]
                    half = slice(part * (S // 2), (part + 1) * (S // 2))
                    if part == 0:
                        full(dve, i, den)
                        full_before(dve, i, ("w1" if x == "a" else "wx", 1))
                    last = v.reciprocal(oT[x][:, n, half], tile(den)[:, half])
                    if part == 1:
                        done(last, den)
                elif kind in ("o1", "ox"):
                    full(dve, i, step)
                    read(dve, i, ("den1" if x == "a" else "denx", n))
                    done(v.tensor_tensor(oT[x][:, n, :], o[:], oT[x][:, n, :], ALU.mult), step)
                elif kind in ("w1", "wx"):
                    dst, res, sig = (x1, xr, xr_done) if kind == "w1" else (x2, x1b, x1b_done)
                    if n == 0:
                        dve.wait_ge(sig.sem, sig.at(i, 1))
                        nxt = x1b_done if kind == "w1" else base_done
                        dve.wait_ge(nxt.sem, nxt.before(i, 1))
                    full(dve, i, step)
                    q = slice(2 * n, 2 * n + 2)
                    done(v.tensor_tensor(dst[:, q, :], o[:].rearrange("p (t d) -> p t d", t=2),
                                         res[:, q, :], ALU.add), step)
                elif kind == "logit":
                    full(dve, i, step)
                    done(v.tensor_tensor(logits[:], o[0:1, 0:8], bp2_row[:], ALU.add), step)
                    v.drain()
                    v.max(top8[:], logits[:])
                    v.drain()
                    v.max_index(sel8[:], top8[:], logits[:]).then_inc(sel_done.sem, 1)
                elif kind == "y3":
                    if n == 0:
                        dve.wait_ge(base_done.sem, base_done.at(i, 1))
                    full(dve, i, step)
                    q = slice(2 * n, 2 * n + 2)
                    done(v.scalar_tensor_tensor(base[:, q, :], o[:].rearrange("p (t d) -> p t d", t=2),
                                                0.3, base[:, q, :], ALU.mult, ALU.add), step)

            def rest():
                v.tensor_scalar(bfo3_row[:], bfo_row[:], 0.3, None, ALU.mult).then_inc(bfo3_done, 1)

            run(dve, body, rest)

        @block.tensor
        def _(pe):
            mm = nc.tensor.matmul
            for sig in filled.values():
                pe.sem_inc(sig.sem, sig.per)
            pe.wait_ge(first_consts_loaded, 16 * len(FIRST_CONSTS))
            pe.wait_ge(pool_consts, 1)

            def chain(dst, pairs):
                for k, (lhsT, rhs) in enumerate(pairs):
                    last = mm(dst, lhsT, rhs, start=(k == 0), stop=(k == len(pairs) - 1))
                return last

            def per_head(dst, lhsT, rhs, w, h):
                for j in range(4):
                    for r in range(2):
                        q = slice(64 * r, 64 * r + 64)
                        last = mm(dst[q, w * j:w * j + w], lhsT[q, 4 * h + j, 0:LM], rhs[q, 4 * h + j, 0:w],
                                  start=True, stop=True)
                return last

            def tokens(n):
                return n // 2, n % 2, slice((n // 2) * P, (n // 2 + 1) * P)

            def body(i, step):
                if step not in BANK:
                    return
                kind, n = step[0], step[1]
                o = tile(step)
                x = "b" if step in IN_B else "a"

                def ready(*steps):
                    need = {BANK[step]: TURN[step]}
                    for m in steps:
                        need[BANK[m]] = max(need.get(BANK[m], 0), TURN[m] + 1)
                    for b, count in need.items():
                        pe.wait_ge(taken[b].sem, taken[b].at(i, count))

                if kind == "kx":
                    ready()
                    pe.wait_ge(ctx_loaded.sem, ctx_loaded.at(i, 32))
                    for m in range(KD):
                        last = chain(o[:, m * LM:(m + 1) * LM],
                                     [(wk[:, k, m * P:(m + 1) * P], ctxT[:, k, :]) for k in range(KD)])
                elif kind == "vx":
                    ready()
                    for r in range(2):
                        last = chain(o[64 * r:64 * r + 64, 0:D],
                                     [(ctxT[:, k, :], wv[:, k, :]) for k in range(KD)])
                elif kind in ("xnTa", "xnTb"):
                    ready()
                    normal = xn_done[x] if n < 2 else xn3_done
                    pe.wait_ge(normal.sem, normal.at(i, 1))
                    for t in range(T):
                        last = nc.tensor.transpose(o[:, t * P:(t + 1) * P],
                                                   xn[x][:, t, (n % 2) * P:(n % 2 + 1) * P], ident[:])
                elif kind in ("q", "k"):
                    ready(("xnTa", 0), ("xnTa", 1))
                    c = (n + 2 * (kind == "k")) * P
                    last = chain(o[:], [(wqkv[:, k, c:c + P], xnT[x][:, k, :]) for k in range(KD)])
                elif kind == "v":
                    ready()
                    for t in range(2):
                        q = slice((2 * n + t) * P, (2 * n + t + 1) * P)
                        last = chain(o[:, t * D:(t + 1) * D],
                                     [(xnT[x][:, k, q], wqkv[:, k, 2 * D:3 * D]) for k in range(KD)])
                elif kind == "s2":
                    ready()
                    pe.wait_ge(bd_done.sem, bd_done.at(i, 2))
                    pe.wait_ge(lm_done.sem, lm_done.at(i, 2))
                    for j in range(PAIRS):
                        last = mm(o[:, j * LM:(j + 1) * LM], pair_of(qbd, j), ksum[:, j // 4, :],
                                  start=True, stop=True)
                elif kind == "s3":
                    ready()
                    if n == 0:
                        pe.wait_ge(bd_done.sem, bd_done.at(i, 1))
                    last = mm(o[:], pair_of(qbd, n), kT[:, n // 4, :], start=True, stop=True)
                elif kind == "x2T":
                    ready()
                    pe.wait_ge(attn2_done.sem, attn2_done.at(i, 1))
                    pe.sem_inc(pe_turn, 1)
                    for j in range(PAIRS):
                        for r in range(2):
                            q = slice(64 * r, 64 * r + 64)
                            last = mm(o[q, j * LM:(j + 1) * LM], attn2[q, j, :], ident[q, q],
                                      start=True, stop=True)
                elif kind == "p3T":
                    ready(("s3", n))
                    for t in range(T):
                        last = nc.tensor.transpose(o[:, t * P:(t + 1) * P],
                                                   p3[:, n % 2, t * P:(t + 1) * P], ident[:])
                elif kind == "a":
                    ready(("x2T", 0))
                    pe.sem_inc(pe_turn, 1)
                    per_head(o, attn2T, attn2, LM, n)
                    last = per_head(o[:, 256:512], attn2, attn2T, LM, n)
                elif kind == "zT":
                    ready(*[("p3T", 4 * n + j) for j in range(4)], ("v", 0), ("v", 1))
                    for t in range(T):
                        for j in range(4):
                            c = (4 * n + j) * 2 * DH
                            last = mm(o[32 * j:32 * j + 32, 0:P], vt[:, t, c:c + 2 * DH], p3T[:, j, t, :],
                                      start=(t == 0), stop=(t == T - 1))
                elif kind == "z":
                    ready(("zT", 0), ("zT", 1))
                    for j in range(2):
                        last = nc.tensor.transpose(o[:, j * P:(j + 1) * P], zT[:, j, :], ident[:])
                elif kind == "ps":
                    it, h = step[1:]
                    if it == 0:
                        ready(("a", h), ("z", 0))
                    else:
                        ready(("put", it - 1, h), ("puz", it - 1, h))
                    pe.sem_inc(pe_turn, 1)
                    last = per_head(o, ut, uz, LM, h)
                elif kind == "pe":
                    it, h = step[1:]
                    ready(("ps", it, h))
                    pe.sem_inc(pe_turn, 1)
                    last = per_head(o, dd, ut, LM, h)
                elif kind == "put":
                    it, h = step[1:]
                    ready(("pe", it, h))
                    pe.sem_inc(pe_turn, 1)
                    last = per_head(o, uz, gt, LM, h)
                elif kind == "puz":
                    it, h = step[1:]
                    ready(("pe", it, h))
                    pe.sem_inc(pe_turn, 1)
                    w = LM + DH
                    if it < ITERS - 1:
                        last = per_head(o, gt, uz, w, h)
                    else:
                        for j in range(4):
                            for r in range(2):
                                q = slice(64 * r, 64 * r + 64)
                                last = mm(o[q, w * j + LM:w * j + w], gt[q, 4 * h + j, :],
                                          uz[q, 4 * h + j, LM:w], start=True, stop=True)
                elif kind == "y":
                    ready(("puz", ITERS - 1, 0), ("puz", ITERS - 1, 1))
                    pe.sem_inc(pe_turn, 1)
                    for j in range(PAIRS):
                        for r in range(2):
                            q = slice(64 * r, 64 * r + 64)
                            last = mm(o[q, j * DH:(j + 1) * DH], attn2T[q, j, :], uz[q, j, LM:LM + DH],
                                      start=True, stop=True)
                elif kind == "s1":
                    ready()
                    if n == 0:
                        pe.wait_ge(bd_done.sem, bd_done.at(i, 4))
                    t, k, q = tokens(n)
                    last = mm(o[:], qT[:, k, q], kbd[:, k].rearrange("p h c -> p (h c)"),
                              start=True, stop=True)
                elif kind in ("p1T", "pxT"):
                    ready()
                    pe.wait_ge(p1_done[x].sem, p1_done[x].at(i, n + 1))
                    pT = p1[x][:, n % SLOTS].rearrange("p h c -> p (h c)")
                    for j in range(4):
                        last = nc.tensor.transpose(o[:, j * P:(j + 1) * P], pT[:, j * P:(j + 1) * P], ident[:])
                elif kind in ("den1", "denx", "o1", "ox"):
                    if kind[0] == "d":
                        turned = "p1T" if x == "a" else "pxT"
                        ready(*[(turned, m) for m in range(8)])
                    else:
                        ready(("y", 0) if x == "a" else ("vx", 0))
                    for j in range(4):
                        w = ones_bd[:] if kind[0] == "d" else (y_bd if x == "a" else vx_bd)[:, 4 * n + j, :]
                        last = mm(o[32 * j:32 * j + 32, :], w, p1T[x][:, 4 * n + j, :], start=True, stop=True)
                elif kind in ("w1", "wx"):
                    ready(*[("o1" if x == "a" else "ox", m) for m in range(2)])
                    for t in range(2):
                        q = slice((2 * n + t) * P, (2 * n + t + 1) * P)
                        w = wout if kind == "w1" else wo
                        last = chain(o[:, t * D:(t + 1) * D],
                                     [(oT[x][:, k, q], w[:, k, :]) for k in range(KD)])
                elif kind == "qx":
                    ready(("xnTb", 0), ("xnTb", 1))
                    last = chain(o[:], [(wq[:, k, n * P:(n + 1) * P], xnT[x][:, k, :]) for k in range(KD)])
                elif kind == "sx":
                    t, k, q = tokens(n)
                    ready(("qx", 0), ("qx", 1))
                    if n == 0:
                        pe.wait_ge(kxbd_done.sem, kxbd_done.at(i, 1))
                    mm(o[:], qxT[:, k, q], kx_bd[:, k].rearrange("p h c -> p (h c)"),
                       start=True, stop=False)
                    last = mm(o[:], ones3[:], neg_row[:].unsqueeze(1).broadcast_to([3, 8, LM]),
                              start=False, stop=True)
                elif kind == "gate":
                    ready(("xnTb", 2), ("xnTb", 3))
                    last = chain(o[:, 0:1], [(wp1[:, k, :], xnT[x][:, k, S - 1:S]) for k in range(KD)])
                elif kind == "logit":
                    ready(("gate", 0))
                    last = mm(o[0:1, 0:8], gate_h[:], wp2[:], start=True, stop=True)
                elif kind == "h":
                    ready()
                    if n == 0:
                        pe.wait_ge(expert_loaded.sem, expert_loaded.at(i, 64))
                    last = chain(o[:], [(w1e[:, k, n * P:(n + 1) * P], xnT[x][:, k, :]) for k in range(KD)])
                elif kind == "r":
                    ready(*[("h", m) for m in range(FM)])
                    last = chain(o[:], [(w2e[:, k, n * P:(n + 1) * P], hT[:, k, :]) for k in range(FM)])
                elif kind == "y3":
                    ready(("r", 0), ("r", 1))
                    for t in range(2):
                        q = slice((2 * n + t) * P, (2 * n + t + 1) * P)
                        last = chain(o[:, t * D:(t + 1) * D],
                                     [(rT[:, k, q], wfo[:, k, :]) for k in range(KD)])
                last.then_inc(filled[stream(step)].sem, 1)

            def pair_of(t, x):
                return t[:, x // 4, 2 * (x % 4):2 * (x % 4) + 2, :].rearrange("p h c -> p (h c)")

            run(pe, body)


def kernel(**inputs):
    import numpy as _np
    import concourse.bacc as _bacc
    from concourse import mybir as _mybir
    from concourse.bass_utils import run_bass_kernel_spmd as _run

    def get(name):
        return _np.asarray(inputs[name])

    def cols(v):
        v = v.reshape(-1, 128)
        return v.T

    def rows(v):
        return _np.broadcast_to(v[None, :], (128, v.shape[0]))

    layout = {
        "x": get("x"),
        "ctxT": get("ctx_1024").transpose(0, 2, 1),
        "mask": rows(get("mask_Bx1x1xS2_ik0").reshape(-1)),
        "Wqkv": get("L0_attn_Wqkv"),
        "bqkv": cols(get("L0_attn_bqkv")),
        "bv": rows(get("L0_attn_bqkv")[512:768]),
        "Wout": get("L0_attn_Wout"),
        "bout": rows(get("L0_attn_bout")),
        "WqT": get("L0_xattn_Wq").T,
        "bqx": cols(get("L0_xattn_bq")),
        "WkT": get("L0_xattn_Wk").T,
        "bkx": cols(get("L0_xattn_bk")),
        "WvT": get("L0_xattn_Wv").T,
        "bvx": rows(get("L0_xattn_bv")),
        "WoT": get("L0_xattn_Wo").T,
        "box": rows(get("L0_xattn_bo")),
        "Wp1": get("L0_ffn_Wp1"),
        "bp1": cols(get("L0_ffn_bp1")),
        "Wp2": get("L0_ffn_Wp2"),
        "bp2": get("L0_ffn_bp2")[None, :],
        "W1": get("L0_ffn_W1"),
        "b1": cols(get("L0_ffn_b1")),
        "W2": get("L0_ffn_W2"),
        "b2": cols(get("L0_ffn_b2")),
        "Wfo": get("L0_ffn_Wo"),
        "bfo": rows(get("L0_ffn_bo")),
    }
    nc = _bacc.Bacc("TRN2", target_bir_lowering=False, num_devices=1)
    arrays, aps = {}, {}
    for name, arr in layout.items():
        arr = _np.ascontiguousarray(arr)
        arrays[f"in_{name}"] = arr
        aps[name] = nc.dram_tensor(f"in_{name}", arr.shape, _mybir.dt.from_np(arr.dtype),
                                   kind="ExternalInput").ap()
    out = nc.dram_tensor("out_0", get("x").shape, _mybir.dt.float32, kind="ExternalOutput").ap()
    decoder_kernel(nc, aps, out)
    r = _run(nc, [arrays], core_ids=[0])
    return r.results[0]["out_0"]
```
